# Optimizing a Trainium2 kernel written in Bass

```python
import numpy as np
import jax
import jax.numpy as jnp

def _softmax(x, axis=-1):
    return jax.nn.softmax(x, axis=axis)

def _gelu(x):
    return jax.nn.gelu(x, approximate=True)

def _silu(x):
    return jax.nn.silu(x)

def _sigmoid(x):
    return jax.nn.sigmoid(x)

def _layernorm(x, axis=-1, eps=1e-05):
    m = jnp.mean(x, axis=axis, keepdims=True)
    v = jnp.var(x, axis=axis, keepdims=True)
    return (x - m) / jnp.sqrt(v + eps)

def _scatter_add(tgt, idx, src, axis=0):
    return tgt.at[idx].add(src)

def _segment_sum(src, seg, n):
    return jax.ops.segment_sum(src, seg, n)
kernel_name = 'mk_xattn_ffn_d2_seqx_r8_073a68'

def setup_inputs(seed: int=0):
    np.random.seed(seed)
    _w = jnp.asarray

    def _rec_inputs():
        import jax
        import jax.numpy as jnp
        _rk = jax.random.key(seed)
        x = 7.22e-05 + 1 * jax.random.normal(jax.random.fold_in(_rk, 1), (16, 128, 128), jnp.float32)
        _lenS = 128 - jax.random.randint(jax.random.fold_in(_rk, 7), (16,), 0, max(1, 128 // 4) + 1, jnp.int32)
        _lenS2 = 128 - jax.random.randint(jax.random.fold_in(_rk, 8), (16,), 0, max(1, 128 // 4) + 1, jnp.int32)
        _ctx_1024P = jax.random.normal(jax.random.fold_in(_rk, 11), (16, 16, 128), jnp.float32)
        _ctx_1024c = jax.random.dirichlet(jax.random.fold_in(_rk, 511), 0.3 * jnp.ones((16,), jnp.float32), (16, 128))
        _ctx_1024t = jnp.einsum('bsk,bkd->bsd', _ctx_1024c, _ctx_1024P)
        _ctx_1024t = _ctx_1024t * jax.lax.rsqrt(jnp.mean(jnp.square(_ctx_1024t)) + 1e-12) * 0.953939
        ctx_1024 = 4.13588e-05 + 0.999923 * (_ctx_1024t + 0.3 * jax.random.normal(jax.random.fold_in(_rk, 611), (16, 128, 128), jnp.float32))
        return (x, ctx_1024)
    x, ctx_1024 = _rec_inputs()

    def _L0_xattn_setup():
        import jax, jax.numpy as jnp
        import numpy as np
        D_MODEL = 128
        NUM_HEADS = 16
        DEPTH = D_MODEL // NUM_HEADS

        def _split_heads(x):
            B, S, _ = x.shape
            return x.reshape(B, S, NUM_HEADS, DEPTH).transpose(0, 2, 1, 3)
        key = jax.random.key(seed)
        ks = jax.random.split(key, 11)
        B, S = (4, 256)
        scale = 1.0 / np.sqrt(D_MODEL)
        inp = {'query': jax.random.normal(ks[0], (B, S, D_MODEL), jnp.float32), 'key': jax.random.normal(ks[1], (B, S, D_MODEL), jnp.float32), 'value': jax.random.normal(ks[2], (B, S, D_MODEL), jnp.float32), 'Wq': jax.random.normal(ks[3], (D_MODEL, D_MODEL), jnp.float32) * scale, 'bq': jnp.zeros((D_MODEL,), jnp.float32), 'Wk': jax.random.normal(ks[4], (D_MODEL, D_MODEL), jnp.float32) * scale, 'bk': jnp.zeros((D_MODEL,), jnp.float32), 'Wv': jax.random.normal(ks[5], (D_MODEL, D_MODEL), jnp.float32) * scale, 'bv': jnp.zeros((D_MODEL,), jnp.float32), 'Wo': jax.random.normal(ks[6], (D_MODEL, D_MODEL), jnp.float32) * scale, 'bo': jnp.zeros((D_MODEL,), jnp.float32)}
        return inp
    _L0_xattn_all = _L0_xattn_setup()
    _L0_xattn_in = {k: v for k, v in _L0_xattn_all.items() if k in ('Wq', 'bq', 'Wk', 'bk', 'Wv', 'bv', 'Wo', 'bo')}
    del _L0_xattn_all

    def _L0_ffn_setup():
        import jax, jax.numpy as jnp
        import numpy as np
        B, T, D, FF, E, TOP_K = (8, 256, 128, 512, 8, 2)
        key = jax.random.key(seed)
        kx, kr, k1, k2 = jax.random.split(key, 4)
        x = jax.random.normal(kx, (B, T, D), dtype=jnp.float32)
        Wr = jax.random.normal(kr, (E, D), dtype=jnp.float32) * 0.02
        W1 = jax.random.normal(k1, (E, D, FF), dtype=jnp.float32) * 0.02
        W2 = jax.random.normal(k2, (E, FF, D), dtype=jnp.float32) * 0.02
        return {'x': x, 'Wr': Wr, 'W1': W1, 'W2': W2}
    _L0_ffn_all = _L0_ffn_setup()
    _L0_ffn_in = {k: v for k, v in _L0_ffn_all.items() if k in ('Wr', 'W1', 'W2')}
    del _L0_ffn_all

    def _L1_xattn_setup():
        import jax, jax.numpy as jnp
        import numpy as np
        C = 128
        B, SQ, SKV = (4, 256, 256)
        key = jax.random.key(seed)
        ks = jax.random.split(key, 10)
        s = 1.0 / np.sqrt(C)
        return {'x': jax.random.normal(ks[0], (B, SQ, C), jnp.float32), 'content_embeddings': jax.random.normal(ks[1], (B, SKV, C), jnp.float32), 'Wq': jax.random.normal(ks[2], (C, C), jnp.float32) * s, 'bq': jnp.zeros((C,), jnp.float32), 'Wk': jax.random.normal(ks[3], (C, C), jnp.float32) * s, 'bk': jnp.zeros((C,), jnp.float32), 'Wv': jax.random.normal(ks[4], (C, C), jnp.float32) * s, 'bv': jnp.zeros((C,), jnp.float32), 'Wo': jax.random.normal(ks[5], (C, C), jnp.float32) * s, 'bo': jnp.zeros((C,), jnp.float32)}
    _L1_xattn_all = _L1_xattn_setup()
    _L1_xattn_in = {k: v for k, v in _L1_xattn_all.items() if k in ('Wq', 'bq', 'Wk', 'bk', 'Wv', 'bv', 'Wo', 'bo')}
    del _L1_xattn_all

    def _L1_ffn_setup():
        import jax, jax.numpy as jnp
        import numpy as np
        DIM = 128
        DEPTH = 6
        HEADS = 16
        DIM_HEAD = 64
        WINDOW = 32
        INNER = HEADS * DIM_HEAD
        DIM_INNER = int(DIM * 4 * 2 / 3)
        QK_SCALE = 8.0

        def shift_tokens(t):
            a, s = jnp.split(t, 2, -1)
            s = jnp.pad(s, ((0, 0), (1, 0), (0, 0)))[:, :-1]
            return jnp.concatenate([a, s], -1)

        def l2norm(t):
            return t / jnp.maximum(jnp.linalg.norm(t, axis=-1, keepdims=True), 1e-12)

        def rotate_half(x):
            x1, x2 = jnp.split(x, 2, -1)
            return jnp.concatenate([-x2, x1], -1)

        def rotary_tables(n):
            half = jnp.arange(0, DIM_HEAD, 2, dtype=jnp.float32)
            inv_freq = 1.0 / 10000.0 ** (half / DIM_HEAD)
            t = jnp.arange(n, dtype=jnp.float32)
            freqs = t[:, None] * inv_freq[None, :]
            freqs = jnp.concatenate([freqs, freqs], -1)
            base_scale = (half + 0.4 * DIM_HEAD) / (1.4 * DIM_HEAD)
            power = (t - n // 2) / (WINDOW // 2)
            scale = base_scale[None, :] ** power[:, None]
            scale = jnp.concatenate([scale, scale], -1)
            return (freqs, scale)

        def local_attention(q, k, v):
            b, h, n, d = q.shape
            w = WINDOW
            nw = n // w
            bq = q.reshape(b, h, nw, w, d)
            bk = k.reshape(b, h, nw, w, d)
            bv = v.reshape(b, h, nw, w, d)

            def look(t):
                p = jnp.pad(t, ((0, 0), (0, 0), (1, 0), (0, 0), (0, 0)))
                return jnp.concatenate([p[:, :, :nw], p[:, :, 1:]], axis=3)
            bk2, bv2 = (look(bk), look(bv))
            seq = jnp.arange(n).reshape(nw, w)
            seq_p = jnp.pad(seq, ((1, 0), (0, 0)), constant_values=-1)
            jt = jnp.concatenate([seq_p[:nw], seq_p[1:]], axis=1)
            it = seq[:, :, None]
            jb = jt[:, None, :]
            mask = (it < jb) | (it > jb + w) | (jb == -1)
            sim = jnp.einsum('bhwie,bhwje->bhwij', bq, bk2) * QK_SCALE
            sim = jnp.where(mask, -jnp.finfo(sim.dtype).max, sim)
            attn = jax.nn.softmax(sim, -1)
            out = jnp.einsum('bhwij,bhwje->bhwie', attn, bv2)
            return out.reshape(b, h, n, d)

        def attn_layer(x, Wqkv, qs, ksc, Wo):
            b, n, _ = x.shape
            qkv = x @ Wqkv
            q, k, v = jnp.split(qkv, 3, -1)
            sh = lambda t: t.reshape(b, n, HEADS, DIM_HEAD).transpose(0, 2, 1, 3)
            q, k, v = (sh(q), sh(k), sh(v))
            q = l2norm(q) * qs
            k = l2norm(k) * ksc
            freqs, scale = rotary_tables(n)
            cos, sin = (jnp.cos(freqs), jnp.sin(freqs))
            q = q * cos * scale + rotate_half(q) * sin * scale
            inv = 1.0 / scale
            k = k * cos * inv + rotate_half(k) * sin * inv
            out = local_attention(q, k, v)
            out = out.transpose(0, 2, 1, 3).reshape(b, n, INNER)
            return out @ Wo

        def ffn_layer(x, g, bln, W1, b1, W2, b2):
            mu = x.mean(-1, keepdims=True)
            var = ((x - mu) ** 2).mean(-1, keepdims=True)
            xn = (x - mu) / jnp.sqrt(var + 1e-05) * g + bln
            hg = xn @ W1 + b1
            a, gate = jnp.split(hg, 2, -1)
            return a * jax.nn.gelu(gate, approximate=False) @ W2 + b2
        key = jax.random.key(seed)
        ks = jax.random.split(key, 8)
        B, N = (2, 256)
        init = lambda k, shape: jax.random.normal(k, shape, jnp.float32) * 0.02
        return {'x': jax.random.normal(ks[0], (B, N, DIM), jnp.float32), 'Wqkv': init(ks[1], (DEPTH, DIM, 3 * INNER)), 'q_scale': jnp.ones((DEPTH, DIM_HEAD), jnp.float32), 'k_scale': jnp.ones((DEPTH, DIM_HEAD), jnp.float32), 'Wo': init(ks[2], (DEPTH, INNER, DIM)), 'ln_g': jnp.ones((DEPTH, DIM), jnp.float32), 'ln_b': jnp.zeros((DEPTH, DIM), jnp.float32), 'W1': init(ks[3], (DEPTH, DIM, 2 * DIM_INNER)), 'b1': jnp.zeros((DEPTH, 2 * DIM_INNER), jnp.float32), 'W2': init(ks[4], (DEPTH, DIM_INNER, DIM)), 'b2': jnp.zeros((DEPTH, DIM), jnp.float32)}
    _L1_ffn_all = _L1_ffn_setup()
    _L1_ffn_in = {k: v for k, v in _L1_ffn_all.items() if k in ('Wqkv', 'q_scale', 'k_scale', 'Wo', 'ln_g', 'ln_b', 'W1', 'b1', 'W2', 'b2')}
    del _L1_ffn_all
    return {'x': x, 'ctx_1024': ctx_1024, 'L0_xattn_Wq': _L0_xattn_in['Wq'], 'L0_xattn_bq': _L0_xattn_in['bq'], 'L0_xattn_Wk': _L0_xattn_in['Wk'], 'L0_xattn_bk': _L0_xattn_in['bk'], 'L0_xattn_Wv': _L0_xattn_in['Wv'], 'L0_xattn_bv': _L0_xattn_in['bv'], 'L0_xattn_Wo': _L0_xattn_in['Wo'], 'L0_xattn_bo': _L0_xattn_in['bo'], 'L0_ffn_Wr': _L0_ffn_in['Wr'], 'L0_ffn_W1': _L0_ffn_in['W1'], 'L0_ffn_W2': _L0_ffn_in['W2'], 'L1_xattn_Wq': _L1_xattn_in['Wq'], 'L1_xattn_bq': _L1_xattn_in['bq'], 'L1_xattn_Wk': _L1_xattn_in['Wk'], 'L1_xattn_bk': _L1_xattn_in['bk'], 'L1_xattn_Wv': _L1_xattn_in['Wv'], 'L1_xattn_bv': _L1_xattn_in['bv'], 'L1_xattn_Wo': _L1_xattn_in['Wo'], 'L1_xattn_bo': _L1_xattn_in['bo'], 'L1_ffn_Wqkv': _L1_ffn_in['Wqkv'], 'L1_ffn_q_scale': _L1_ffn_in['q_scale'], 'L1_ffn_k_scale': _L1_ffn_in['k_scale'], 'L1_ffn_Wo': _L1_ffn_in['Wo'], 'L1_ffn_ln_g': _L1_ffn_in['ln_g'], 'L1_ffn_ln_b': _L1_ffn_in['ln_b'], 'L1_ffn_W1': _L1_ffn_in['W1'], 'L1_ffn_b1': _L1_ffn_in['b1'], 'L1_ffn_W2': _L1_ffn_in['W2'], 'L1_ffn_b2': _L1_ffn_in['b2']}

def reference(x, ctx_1024, L0_xattn_Wq, L0_xattn_bq, L0_xattn_Wk, L0_xattn_bk, L0_xattn_Wv, L0_xattn_bv, L0_xattn_Wo, L0_xattn_bo, L0_ffn_Wr, L0_ffn_W1, L0_ffn_W2, L1_xattn_Wq, L1_xattn_bq, L1_xattn_Wk, L1_xattn_bk, L1_xattn_Wv, L1_xattn_bv, L1_xattn_Wo, L1_xattn_bo, L1_ffn_Wqkv, L1_ffn_q_scale, L1_ffn_k_scale, L1_ffn_Wo, L1_ffn_ln_g, L1_ffn_ln_b, L1_ffn_W1, L1_ffn_b1, L1_ffn_W2, L1_ffn_b2):
    import jax
    import jax.numpy as jnp

    def _L0_xattn_ref(query, key, value, Wq, bq, Wk, bk, Wv, bv, Wo, bo):
        import jax, jax.numpy as jnp
        import numpy as np
        D_MODEL = 128
        NUM_HEADS = 16
        DEPTH = D_MODEL // NUM_HEADS

        def _split_heads(x):
            B, S, _ = x.shape
            return x.reshape(B, S, NUM_HEADS, DEPTH).transpose(0, 2, 1, 3)
        B, S, _ = query.shape
        q = _split_heads(query @ Wq + bq)
        k = _split_heads(key @ Wk + bk)
        v = _split_heads(value @ Wv + bv)
        logits = jnp.einsum('bhqd,bhkd->bhqk', q, k) / jnp.sqrt(jnp.float32(DEPTH))
        attn = jax.nn.softmax(logits, axis=-1)
        out = jnp.einsum('bhqk,bhkd->bhqd', attn, v)
        out = out.transpose(0, 2, 1, 3).reshape(B, S, D_MODEL)
        return out @ Wo + bo

    def _L0_ffn_ref(x, Wr, W1, W2):
        import jax, jax.numpy as jnp
        import numpy as np
        B, T, D, FF, E, TOP_K = (8, 256, 128, 512, 8, 2)
        Bs, Ts, Ds = x.shape
        Ne = Wr.shape[0]
        xf = x.reshape(-1, Ds)
        N = xf.shape[0]
        logits = xf @ Wr.T
        topk_vals, topk_idx = jax.lax.top_k(logits, TOP_K)
        w = jax.nn.softmax(topk_vals.astype(jnp.float32), axis=-1).astype(x.dtype)
        idx_flat = topk_idx.reshape(-1)
        w_flat = w.reshape(-1)
        sort_idx = jnp.argsort(idx_flat)
        rev = sort_idx // TOP_K
        sw = w_flat[sort_idx]
        perm = xf[rev]
        S = perm.shape[0]
        chunks = perm.reshape(Ne, S // Ne, Ds)
        h = jax.nn.gelu(jnp.einsum('ecd,edf->ecf', chunks, W1), approximate=False)
        eo = jnp.einsum('ecf,efd->ecd', h, W2).reshape(S, Ds)
        out = jnp.zeros((N, Ds), dtype=x.dtype).at[rev].add(eo * sw[:, None])
        return out.reshape(Bs, Ts, Ds)

    def _L1_xattn_ref(x, content_embeddings, Wq, bq, Wk, bk, Wv, bv, Wo, bo):
        import jax, jax.numpy as jnp
        import numpy as np
        C = 128
        B, SQ, SKV = (4, 256, 256)
        queries = x @ Wq.T + bq
        keys = content_embeddings @ Wk.T + bk
        values = content_embeddings @ Wv.T + bv
        scale = 1.0 / jnp.sqrt(jnp.asarray(C, x.dtype))
        scores = jnp.einsum('bqc,bkc->bqk', queries, keys) * scale
        attn = jax.nn.softmax(scores, axis=-1)
        attended = jnp.einsum('bqk,bkc->bqc', attn, values)
        out = x + attended
        return out @ Wo.T + bo

    def _L1_ffn_ref(x, Wqkv, q_scale, k_scale, Wo, ln_g, ln_b, W1, b1, W2, b2):
        import jax, jax.numpy as jnp
        import numpy as np
        DIM = 128
        DEPTH = 6
        HEADS = 16
        DIM_HEAD = 64
        WINDOW = 32
        INNER = HEADS * DIM_HEAD
        DIM_INNER = int(DIM * 4 * 2 / 3)
        QK_SCALE = 8.0

        def shift_tokens(t):
            a, s = jnp.split(t, 2, -1)
            s = jnp.pad(s, ((0, 0), (1, 0), (0, 0)))[:, :-1]
            return jnp.concatenate([a, s], -1)

        def l2norm(t):
            return t / jnp.maximum(jnp.linalg.norm(t, axis=-1, keepdims=True), 1e-12)

        def rotate_half(x):
            x1, x2 = jnp.split(x, 2, -1)
            return jnp.concatenate([-x2, x1], -1)

        def rotary_tables(n):
            half = jnp.arange(0, DIM_HEAD, 2, dtype=jnp.float32)
            inv_freq = 1.0 / 10000.0 ** (half / DIM_HEAD)
            t = jnp.arange(n, dtype=jnp.float32)
            freqs = t[:, None] * inv_freq[None, :]
            freqs = jnp.concatenate([freqs, freqs], -1)
            base_scale = (half + 0.4 * DIM_HEAD) / (1.4 * DIM_HEAD)
            power = (t - n // 2) / (WINDOW // 2)
            scale = base_scale[None, :] ** power[:, None]
            scale = jnp.concatenate([scale, scale], -1)
            return (freqs, scale)

        def local_attention(q, k, v):
            b, h, n, d = q.shape
            w = WINDOW
            nw = n // w
            bq = q.reshape(b, h, nw, w, d)
            bk = k.reshape(b, h, nw, w, d)
            bv = v.reshape(b, h, nw, w, d)

            def look(t):
                p = jnp.pad(t, ((0, 0), (0, 0), (1, 0), (0, 0), (0, 0)))
                return jnp.concatenate([p[:, :, :nw], p[:, :, 1:]], axis=3)
            bk2, bv2 = (look(bk), look(bv))
            seq = jnp.arange(n).reshape(nw, w)
            seq_p = jnp.pad(seq, ((1, 0), (0, 0)), constant_values=-1)
            jt = jnp.concatenate([seq_p[:nw], seq_p[1:]], axis=1)
            it = seq[:, :, None]
            jb = jt[:, None, :]
            mask = (it < jb) | (it > jb + w) | (jb == -1)
            sim = jnp.einsum('bhwie,bhwje->bhwij', bq, bk2) * QK_SCALE
            sim = jnp.where(mask, -jnp.finfo(sim.dtype).max, sim)
            attn = jax.nn.softmax(sim, -1)
            out = jnp.einsum('bhwij,bhwje->bhwie', attn, bv2)
            return out.reshape(b, h, n, d)

        def attn_layer(x, Wqkv, qs, ksc, Wo):
            b, n, _ = x.shape
            qkv = x @ Wqkv
            q, k, v = jnp.split(qkv, 3, -1)
            sh = lambda t: t.reshape(b, n, HEADS, DIM_HEAD).transpose(0, 2, 1, 3)
            q, k, v = (sh(q), sh(k), sh(v))
            q = l2norm(q) * qs
            k = l2norm(k) * ksc
            freqs, scale = rotary_tables(n)
            cos, sin = (jnp.cos(freqs), jnp.sin(freqs))
            q = q * cos * scale + rotate_half(q) * sin * scale
            inv = 1.0 / scale
            k = k * cos * inv + rotate_half(k) * sin * inv
            out = local_attention(q, k, v)
            out = out.transpose(0, 2, 1, 3).reshape(b, n, INNER)
            return out @ Wo

        def ffn_layer(x, g, bln, W1, b1, W2, b2):
            mu = x.mean(-1, keepdims=True)
            var = ((x - mu) ** 2).mean(-1, keepdims=True)
            xn = (x - mu) / jnp.sqrt(var + 1e-05) * g + bln
            hg = xn @ W1 + b1
            a, gate = jnp.split(hg, 2, -1)
            return a * jax.nn.gelu(gate, approximate=False) @ W2 + b2
        for i in range(DEPTH):
            x = attn_layer(shift_tokens(x), Wqkv[i], q_scale[i], k_scale[i], Wo[i]) + x
            x = ffn_layer(shift_tokens(x), ln_g[i], ln_b[i], W1[i], b1[i], W2[i], b2[i]) + x
        return x
    x = x + _L0_xattn_ref(_layernorm(x, axis=-1), ctx_1024, ctx_1024, L0_xattn_Wq, L0_xattn_bq, L0_xattn_Wk, L0_xattn_bk, L0_xattn_Wv, L0_xattn_bv, L0_xattn_Wo, L0_xattn_bo)
    x = x + _L0_ffn_ref(_layernorm(x, axis=-1), L0_ffn_Wr, L0_ffn_W1, L0_ffn_W2)
    x = x + _L1_xattn_ref(_layernorm(x, axis=-1), ctx_1024, L1_xattn_Wq, L1_xattn_bq, L1_xattn_Wk, L1_xattn_bk, L1_xattn_Wv, L1_xattn_bv, L1_xattn_Wo, L1_xattn_bo)
    x = x + _L1_ffn_ref(_layernorm(x, axis=-1), L1_ffn_Wqkv, L1_ffn_q_scale, L1_ffn_k_scale, L1_ffn_Wo, L1_ffn_ln_g, L1_ffn_ln_b, L1_ffn_W1, L1_ffn_b1, L1_ffn_W2, L1_ffn_b2)
    return x

_drawn_inputs = setup_inputs


def setup_inputs(seed=0):
    import zlib

    import numpy as np

    out = dict(_drawn_inputs(seed))
    spreads = {'L0_xattn_bq': (0.0, 0.352),
     'L0_xattn_bk': (0.0, 0.8),
     'L0_xattn_bv': (0.0, 0.1),
     'L0_xattn_bo': (0.0, 0.1),
     'L1_xattn_bq': (0.0, 0.478),
     'L1_xattn_bk': (0.0, 0.8),
     'L1_xattn_bv': (0.0, 0.1),
     'L1_xattn_bo': (0.0, 0.1),
     'L1_ffn_q_scale': (1.0, 0.6),
     'L1_ffn_k_scale': (1.0, 0.6),
     'L1_ffn_ln_g': (1.0, 0.6),
     'L1_ffn_ln_b': (0.0, 0.8),
     'L1_ffn_b1': (0.0, 0.8),
     'L1_ffn_b2': (0.0, 0.1)}
    factors = {'L1_ffn_W1': 4.749, 'L1_ffn_W2': 4.691}
    for name, (base, spread) in spreads.items():
        noise = np.random.default_rng([zlib.crc32(name.encode()), seed]).standard_normal(out[name].shape)
        drawn = base * np.exp(spread * noise) if base else spread * noise
        out[name] = jnp.asarray(drawn.astype(out[name].dtype))
    for name, factor in factors.items():
        out[name] = (out[name] * factor).astype(out[name].dtype)
    return out
```

```python
from contextlib import ExitStack

import numpy as np

import concourse.bass as bass
from concourse import mybir

F32 = mybir.dt.float32
BF16 = mybir.dt.bfloat16
I32 = mybir.dt.int32
U32 = mybir.dt.uint32
ALU = mybir.AluOpType
ACT = mybir.ActivationFunctionType
AX = mybir.AxisListType

P = 128
B = 16
D = 128
HEADS = 16
UH = HEADS // 2
UNITS = 2 * B
BANK = 512
LN_EPS = 1e-5
FLT_MAX = float(np.finfo(np.float32).max)

DEPTH0 = D // HEADS
SCALE0 = float(DEPTH0) ** -0.5

EXPERTS = 8
FF = 512
TOPK = 2
ROWS = B * P * TOPK
CHUNK = ROWS // EXPERTS

SCALE1 = float(D) ** -0.5

LAYERS = 6
DH = 64
INNER = HEADS * DH
WINDOW = 32
GLU = 341
GCH = [(0, 128), (128, 128), (256, GLU - 256)]
QK_SCALE = 8.0
QUAD = 4
QUADS = B // QUAD


def units(eng, body, ahead):
    for i in range(4):
        body(i // 2, i, i, lambda k: i >= k)
    with eng.Fori(2, B - 3, 2) as b0:
        for s in range(4):
            body(b0 + s // 2, b0 * 2 + s, s, lambda k: True)
    for i in range(UNITS - 4, UNITS + ahead):
        body(i // 2, i, i % 4, lambda k: i - k < UNITS)


def one(b):
    return bass.ds(b, 1)


def row(ap):
    return ap.rearrange("p o d -> p (o d)")


class Core:

    def __init__(self, nc, ctx, io):
        self.nc, self.io = nc, io
        self.sems = ctx
        sb = lambda name, shape, dt=F32: ctx.enter_context(nc.sbuf_tensor(name, shape, dt))
        self.X = sb("X", [P, B, D])
        self.ident = sb("ident", [P, P])
        self.stats = sb("ln_stats", [P, B, 6])
        self.meanvar = sb("ln_meanvar", [P, B, 2])
        self.vareps = sb("ln_vareps", [P, B])
        self.rstd = sb("ln_rstd", [P, B])
        self.minus_half = sb("minus_half", [P, B])

    def sem(self, name):
        return self.sems.enter_context(self.nc.semaphore(name))


def ln_stats_dve(dve, c, stats_done, ln_step, X):
    for b in range(B):
        dve.bn_stats(c.stats[:, b, :], X[:, b, :]).then_inc(stats_done, 1)
    dve.wait_ge(stats_done, B)
    for b in range(B):
        dve.bn_aggr(c.meanvar[:, b, :], c.stats[:, b, :]).then_inc(stats_done, 1)
    dve.wait_ge(stats_done, 2 * B)
    dve.tensor_scalar(c.vareps[:, :], c.meanvar[:, :, 1], LN_EPS, None, ALU.add).then_inc(ln_step, 1)


def ln_rstd_pool(pool, c, ln_step, rstd_done):
    pool.memset(c.minus_half[:, :], -0.5).then_inc(rstd_done, 1)
    pool.wait_ge(rstd_done, 1)
    pool.wait_ge(ln_step, 1)
    pool.tensor_tensor(c.rstd[:, :], c.vareps[:, :], c.minus_half[:, :], ALU.pow).then_inc(rstd_done, 1)


def first_attention(c):
    nc, io = c.nc, c.io
    with ExitStack() as ctx:
        sb = lambda name, shape, dt=F32: ctx.enter_context(nc.sbuf_tensor("a_" + name, shape, dt))
        ps = lambda name, shape, dt=F32: ctx.enter_context(nc.psum_tensor("a_" + name, shape, dt))
        sem = lambda name: c.sem("a_" + name)
        X = c.X
        w_raw = sb("w_raw", [P, 2, D])
        w_pad = sb("w_pad", [P, 2, 4, P])
        b_pad = sb("b_pad", [P, 2, 2, 2])
        bv_all = sb("bv_all", [P, D])
        bo_all = sb("bo_all", [P, D])
        ctx_in = sb("ctx_in", [P, 2, D])
        xn_in = sb("xn_in", [P, 2, D])
        xcT = sb("xcT", [P, 2, 2, P])
        qkT = sb("qkT", [P, 2, 4, P])
        v1 = sb("v1", [P, 2, HEADS, DEPTH0 + 1])
        mx = sb("mx", [P, 2, UH])
        sd = sb("sd", [P, 2, UH, P])
        pr = sb("pr", [P, 2, UH, P])
        prT = sb("prT", [P, UH, P])
        rden = sb("rden", [P, UH])
        on = sb("on", [P, 2, D])
        onT = sb("onT", [P, D])
        proj = sb("proj", [P, D])

        psT = ps("psT", [P, BANK])
        psP = ps("psP", [P, 4, P])
        psPT = ps("psPT", [P, 4, P])
        psO = ps("psO", [P, BANK])
        psS = ps("psS", [P, 4, 4, P])
        OW = UH * (DEPTH0 + 1)

        ld_w, ld_x, ld_ctx = sem("ld_w"), sem("ld_x"), [sem("ld_ctx0"), sem("ld_ctx1")]
        vones = sem("vones")
        stats_done, ln_step, rstd_done = sem("stats_done"), sem("ln_step"), sem("rstd_done")
        xn_ready, t_done, xcT_ready = sem("xn_ready"), sem("t_done"), sem("xcT_ready")
        qk_proj, qk_ready, v_proj, v_ready = sem("qk_proj"), sem("qk_ready"), sem("v_proj"), sem("v_ready")
        s_done, mx_done, sd_done, exp_done = sem("s_done"), sem("mx_done"), sem("sd_done"), sem("exp_done")
        pt_done, pt_ready, pv_done, rden_done = sem("pt_done"), sem("pt_ready"), sem("pv_done"), sem("rden_done")
        on_done, onT_done, onT_ready = sem("on_done"), sem("onT_done"), sem("onT_ready")
        wo_done, proj_done, x_done = sem("wo_done"), sem("proj_done"), sem("x_done")

        block = ctx.enter_context(nc.Block())

        @block.sync
        def _(sp):
            sp.dma_start(X[:, :, :], io["x"].rearrange("b t d -> t b d")).then_inc(ld_x, 16)
            sp.dma_start(c.ident[:, :], io["c_ident"]).then_inc(ld_w, 16)
            sp.dma_start(w_pad[:, :, :, :], io["l_w0_pad"]).then_inc(ld_w, 16)
            sp.dma_start(b_pad[:, :, :, :], io["l_b0_pad"]).then_inc(ld_w, 16)
            for n, w in enumerate(("Wv", "Wo")):
                sp.dma_start(w_raw[:, n, :], io["L0_xattn_" + w]).then_inc(ld_w, 16)
            for b in range(2):
                sp.dma_start(ctx_in[:, b, :], io["ctx_1024"][b]).then_inc(ld_ctx[b], 16)
            sp.dma_start(bv_all[:, :], io["L0_xattn_bv"].partition_broadcast(P)).then_inc(ld_w, 16)
            sp.dma_start(bo_all[:, :], io["L0_xattn_bo"].partition_broadcast(P)).then_inc(ld_w, 16)
            with sp.Fori(0, B - 3, 2) as b0:
                for p in range(2):
                    sp.wait_ge(t_done, b0 + p + 1)
                    sp.dma_start(ctx_in[:, p, :], io["ctx_1024"][bass.ds(b0 + p + 2, 1), :, :]
                                 .rearrange("o t d -> t (o d)")).then_inc(ld_ctx[p], 16)

        @block.gpsimd
        def _(pool):
            pool.memset(v1[:, :, :, DEPTH0:], 1.0).then_inc(vones, 1)
            ln_rstd_pool(pool, c, ln_step, rstd_done)

        @block.vector
        def _(dve):
            dve.wait_ge(ld_x, 16)
            ln_stats_dve(dve, c, stats_done, ln_step, X)
            dve.wait_ge(ld_w, 16 * 7)
            dve.wait_ge(rstd_done, 2)

            def stage(b, pb):
                dve.tensor_scalar(xn_in[:, pb, :], row(X[:, one(b), :]), c.meanvar[:, one(b), 0],
                                  c.rstd[:, one(b)], ALU.subtract, ALU.mult).then_inc(xn_ready, 1)

            stage(0, 0)
            dve.wait_ge(vones, 1)

            def body(b, i, s, live):
                half, pb = s % 2, s // 2
                if live(4) and s % 2 == 1:
                    dve.wait_ge(wo_done, b - 1)
                    dve.tensor_tensor(proj[:, :], psO[:, 0:D], bo_all[:, :], ALU.add)\
                       .then_inc(proj_done, 1)
                    dve.wait_ge(proj_done, b - 1)
                    dve.tensor_tensor(row(X[:, one(b - 2), :]), proj[:, :], row(X[:, one(b - 2), :]),
                                      ALU.add).then_inc(x_done, 1)
                if live(0):
                    dve.wait_ge(qk_proj, i + 1)
                    dve.tensor_tensor(qkT[:, half, :, :], psP[:, :, :],
                                      b_pad[:, half, :, :].rearrange("p a g -> p (a g)").unsqueeze(2)
                                      .to_broadcast([P, 4, P]), ALU.add).then_inc(qk_ready, 1)
                    if half == 0:
                        dve.wait_ge(v_proj, b + 1)
                        dve.tensor_tensor(v1[:, pb, :, 0:DEPTH0],
                                          psO[:, 0:D].rearrange("p (n d) -> p n d", d=DEPTH0),
                                          bv_all[:, :].rearrange("p (n d) -> p n d", d=DEPTH0),
                                          ALU.add).then_inc(v_ready, 1)
                    elif live(-1):
                        if live(2):
                            dve.wait_ge(t_done, b)
                        stage(b + 1, 1 - pb)
                if live(1):
                    u = (s - 1) % 2
                    dve.wait_ge(s_done, i)
                    dve.tensor_reduce(mx[:, u, :].rearrange("p (h g) -> p h g", h=4), psS[:, :, 0:2, :],
                                      AX.X, ALU.max).then_inc(mx_done, 1)
                    dve.wait_ge(mx_done, i)
                    dve.tensor_tensor(sd[:, u, :, :].rearrange("p (h g) k -> p h g k", h=4), psS[:, :, 0:2, :],
                                      mx[:, u, :].rearrange("p (h g) -> p h g", h=4).unsqueeze(3)
                                      .to_broadcast([P, 4, 2, P]), ALU.subtract).then_inc(sd_done, 1)
                if live(2):
                    u, q = s % 2, ((s - 2) % 4) // 2
                    o = psO[:, 0:OW].rearrange("p (n d) -> p n d", d=DEPTH0 + 1)
                    dve.wait_ge(pv_done, i - 1)
                    dve.reciprocal(rden[:, :], o[:, :, DEPTH0]).then_inc(rden_done, 1)
                    dve.wait_ge(rden_done, i - 1)
                    dve.tensor_tensor(on[:, q, 64 * u:64 * u + 64].rearrange("p (n d) -> p n d", d=DEPTH0),
                                      o[:, :, 0:DEPTH0],
                                      rden[:, :].unsqueeze(2).to_broadcast([P, UH, DEPTH0]),
                                      ALU.mult).then_inc(on_done, 1)

            units(dve, body, 4)
            dve.wait_ge(x_done, B)

        @block.scalar
        def _(act):
            def evac_xc(b, pb):
                act.wait_ge(t_done, b + 1)
                act.activation(xcT[:, pb, :, :].rearrange("p a t -> p (a t)"), psT[:, 0:256], ACT.Copy)\
                   .then_inc(xcT_ready, 1)

            evac_xc(0, 0)

            def body(b, i, s, live):
                half, pb = s % 2, s // 2
                if live(0) and half == 1 and live(-1):
                    evac_xc(b + 1, 1 - pb)
                if live(2):
                    for part in range(2):
                        act.wait_ge(pt_done, i * 2 - 3 + part)
                        act.activation(prT[:, 4 * part:4 * part + 4, :], psPT[:, :, :], ACT.Copy)\
                           .then_inc(pt_ready, 1)
                if live(1):
                    u = (s - 1) % 2
                    act.wait_ge(sd_done, i)
                    act.activation(pr[:, u, :, :], sd[:, u, :, :], ACT.Exp, scale=SCALE0).then_inc(exp_done, 1)
                if live(3) and s % 2 == 0:
                    act.wait_ge(onT_done, b - 1)
                    act.activation(onT[:, :], psT[:, 0:D], ACT.Copy).then_inc(onT_ready, 1)

            units(act, body, 4)

        @block.tensor
        def _(pe):
            pe.wait_ge(ld_w, 16 * 7)

            def transposes(b, pb):
                pe.wait_ge(xn_ready, b + 1)
                pe.wait_ge(ld_ctx[pb], b * 8 + 16 - 8 * pb)
                pe.transpose(psT[:, 0:128], xn_in[:, pb, :], c.ident[:, :])
                pe.transpose(psT[:, 128:256], ctx_in[:, pb, :], c.ident[:, :]).then_inc(t_done, 1)

            transposes(0, 0)

            def body(b, i, s, live):
                half, pb = s % 2, s // 2
                if live(4) and s % 2 == 1:
                    pe.wait_ge(onT_ready, b - 1)
                    if live(3):
                        pe.wait_ge(on_done, i - 2)
                    pe.matmul(psO[:, 0:D], onT[:, :], w_raw[:, 1, :],
                              start=True, stop=True).then_inc(wo_done, 1)
                if live(0):
                    pe.wait_ge(xcT_ready, b + 1)
                    if live(1):
                        pe.wait_ge(qk_ready, i)
                    for qk in range(2):
                        for g in range(2):
                            mm = pe.matmul(psP[:, 2 * qk + g, :], w_pad[:, qk, 2 * half + g, :],
                                           xcT[:, pb, qk, :], start=True, stop=True)
                    mm.then_inc(qk_proj, 1)
                    if half == 0:
                        if live(3):
                            pe.wait_ge(on_done, i - 2)
                        pe.matmul(psO[:, 0:D], xcT[:, pb, 1, :], w_raw[:, 0, :],
                                  start=True, stop=True).then_inc(v_proj, 1)
                    elif live(-1):
                        if live(4):
                            pe.wait_ge(onT_ready, b - 1)
                        transposes(b + 1, 1 - pb)
                if live(1):
                    u = (s - 1) % 2
                    pe.wait_ge(qk_ready, i)
                    if live(2):
                        pe.wait_ge(sd_done, i - 1)
                    for g in range(2):
                        for blk in range(4):
                            r = slice(32 * blk, 32 * blk + 32)
                            mm = pe.matmul(psS[:, blk, g, :], qkT[r, u, g, :], qkT[r, u, 2 + g, :],
                                           start=True, stop=True)
                    mm.then_inc(s_done, 1)
                if live(2):
                    u, q = s % 2, ((s - 2) % 4) // 2
                    pe.wait_ge(exp_done, i - 1)
                    for part in range(2):
                        if part == 1:
                            pe.wait_ge(pt_ready, i * 2 - 3)
                        for n in range(4):
                            mm = pe.transpose(psPT[:, n, :], pr[:, u, 4 * part + n, :], c.ident[:, :])
                        mm.then_inc(pt_done, 1)
                    pe.wait_ge(pt_ready, i * 2 - 2)
                    if s % 2 == 0:
                        if live(0):
                            pe.wait_ge(v_ready, b + 1)
                    elif live(4):
                        pe.wait_ge(proj_done, b - 1)
                    if live(3):
                        pe.wait_ge(on_done, i - 2)
                    for blk in range(4):
                        for g in range(2):
                            n = 4 * g + blk
                            mm = pe.matmul(psO[:, n * 9:n * 9 + 9], prT[:, 2 * blk + g, :],
                                           v1[:, q, UH * u + n, :], start=True, stop=True)
                    mm.then_inc(pv_done, 1)
                if live(3) and s % 2 == 0:
                    pe.wait_ge(on_done, i - 2)
                    pe.transpose(psT[:, 0:D], on[:, ((s - 3) % 4) // 2, :], c.ident[:, :]).then_inc(onT_done, 1)
            units(pe, body, 4)


def expert_ffn(c):
    nc, io = c.nc, c.io
    with ExitStack() as ctx:
        sb = lambda name, shape, dt=F32: ctx.enter_context(nc.sbuf_tensor("b_" + name, shape, dt))
        ps = lambda name, shape, dt=F32: ctx.enter_context(nc.psum_tensor("b_" + name, shape, dt))
        sem = lambda name: c.sem("b_" + name)
        X, E, T4 = c.X, EXPERTS, CHUNK // P
        sorted_rows = nc.dram_tensor("b_sorted_rows", [ROWS, D], F32, kind="Internal").ap()
        expert_out = nc.dram_tensor("b_expert_out", [ROWS, D], F32, kind="Internal").ap()

        xn = sb("xn", [P, B, D])
        xnT = sb("xnT", [P, 2, QUAD, P])
        wrT = sb("wrT", [P, E])
        before = sb("before", [P, P])
        ones = sb("ones", [P, P])
        lower = sb("lower", [P, E, E])
        lg = sb("lg", [P, B, E])
        gt = sb("gt", [P, B, E, E])
        eq = sb("eq", [P, B, E, E])
        eql = sb("eql", [P, B, E, E])
        cnt = sb("cnt", [P, B, E, E])
        rank = sb("rank", [P, B, E])
        chosen = sb("chosen", [P, B, E])
        sel = sb("sel", [P, 2, B, E])
        tot = sb("tot", [P, E, B])
        scan = sb("scan", [P, E * B])
        start = sb("start", [P, E, B])
        pos = sb("pos", [P, B, E])
        pick = sb("pick", [P, 2, 2, B, E])
        picked = sb("picked", [P, 2, 2, B])
        where = sb("where", [P, 2, B], U32)
        dl = sb("dl", [P, B])
        ex = sb("ex", [P, B])
        den = sb("den", [P, B])
        wt = sb("wt", [P, 2, B])

        rows = sb("rows", [P, 2, T4, P])
        w1 = sb("w1", [P, 2, FF])
        w2 = sb("w2", [P, 2, FF // P, D])
        rowsT = sb("rowsT", [P, CHUNK])
        hid = sb("hid", [P, 2, FF // P, CHUNK])
        eo = sb("eo", [P, 2, T4 * D])
        got = sb("got", [P, 2, B, D])

        psT = ps("psT", [P, 4, P])
        psL = ps("psL", [P, BANK])
        psC = ps("psC", [P, BANK])
        psH = ps("psH", [P, FF // P, BANK])
        psY = ps("psY", [P, BANK])

        ld_c, ld_w, ld_r = sem("ld_c"), [sem("ld_w0"), sem("ld_w1")], [sem("ld_r0"), sem("ld_r1")]
        stats_done, ln_step, rstd_done = sem("stats_done"), sem("ln_step"), sem("rstd_done")
        xn_done, t_done, xnT_ready, lg_done = sem("xn_done"), sem("t_done"), sem("xnT_ready"), sem("lg_done")
        route = sem("route")
        choice_ready, count_done, dl_ready, ex_done = sem("choice_ready"), sem("count_done"), sem("dl_ready"), sem("ex_done")
        where_ready, scattered = sem("where_ready"), sem("scattered")
        rT_done, rT_ready, up_done, hid_ready = sem("rT_done"), sem("rT_ready"), sem("up_done"), sem("hid_ready")
        down_done, eo_ready, eo_out = sem("down_done"), sem("eo_ready"), [sem("eo_out0"), sem("eo_out1")]
        gathered, x_step = sem("gathered"), sem("x_step")

        block = ctx.enter_context(nc.Block())

        @block.sync
        def _(sp):
            sp.dma_start(wrT[:, :], io["l_wr"]).then_inc(ld_c, 16)
            sp.dma_start(before[:, :], io["c_before"]).then_inc(ld_c, 16)
            sp.dma_start(lower[:, :, :], io["c_lower"].partition_broadcast(P)).then_inc(ld_c, 16)

            def load_weights(e, p):
                sp.dma_start(w1[:, p, :], io["L0_ffn_W1"][one(e), :, :].rearrange("o k n -> k (o n)"))\
                  .then_inc(ld_w[p], 16)
                sp.dma_start(w2[:, p, :, :], io["L0_ffn_W2"][one(e), :, :].rearrange("o (c k) n -> k (o c) n", k=P))\
                  .then_inc(ld_w[p], 16)

            def load_rows(e, p):
                src = sorted_rows.rearrange("(e t p) d -> e p t d", e=E, p=P)
                sp.dma_start(rows[:, p, :, :], src[one(e), :, :, :].rearrange("o p t d -> p (o t) d"))\
                  .then_inc(ld_r[p], 16)

            def store_out(e, p):
                dst = expert_out.rearrange("(e t p) d -> e p t d", e=E, p=P)
                sp.dma_start(dst[one(e), :, :, :].rearrange("o p t d -> p (o t) d"),
                             eo[:, p, :].rearrange("p (t d) -> p t d", d=D)).then_inc(eo_out[p], 16)

            for e in range(2):
                load_weights(e, e)
            sp.wait_ge(scattered, 16 * TOPK * B)
            for e in range(2):
                load_rows(e, e)
            with sp.Fori(0, E - 3, 2) as e0:
                for p in range(2):
                    sp.wait_ge(rT_done, e0 + p + 1)
                    load_rows(e0 + p + 2, p)
                    sp.wait_ge(down_done, e0 + p + 1)
                    load_weights(e0 + p + 2, p)
                    sp.wait_ge(eo_ready, e0 + p + 1)
                    store_out(e0 + p, p)
            for e in range(E - 2, E):
                sp.wait_ge(eo_ready, e + 1)
                store_out(e, e % 2)
            for p in range(2):
                sp.wait_ge(eo_out[p], 16 * E // 2)

        @block.gpsimd
        def _(pool):
            pool.memset(ones[:, :], 1.0).then_inc(ld_c, 16)
            ln_rstd_pool(pool, c, ln_step, rstd_done)
            pool.wait_ge(xn_done, B)
            for b in range(B):
                for k in range(TOPK):
                    pool.wait_ge(where_ready, 2)
                    pool.indirect_dma_start(
                        out=sorted_rows, out_offset=bass.IndirectOffsetOnAxis(ap=where[:, k, b:b + 1], axis=0),
                        in_=xn[:, b, :], in_offset=None).then_inc(scattered, 16)
            for p in range(2):
                pool.wait_ge(eo_out[p], 16 * E // 2)
            for b in range(B):
                for k in range(TOPK):
                    pool.indirect_dma_start(
                        out=got[:, k, b, :], out_offset=None, in_=expert_out,
                        in_offset=bass.IndirectOffsetOnAxis(ap=where[:, k, b:b + 1], axis=0)).then_inc(gathered, 16)

        @block.vector
        def _(dve):
            ln_stats_dve(dve, c, stats_done, ln_step, X)
            dve.wait_ge(rstd_done, 2)
            for b in range(B):
                dve.tensor_scalar(xn[:, b, :], X[:, b, :], c.meanvar[:, b, 0:1], c.rstd[:, b:b + 1],
                                  ALU.subtract, ALU.mult).then_inc(xn_done, 1)

            steps = [0]

            def then(ins):
                steps[0] += 1
                ins.then_inc(route, 1)
                dve.wait_ge(route, steps[0])

            dve.wait_ge(lg_done, B)
            dve.wait_ge(ld_c, 64)
            then(dve.tensor_copy(lg[:, :, :].rearrange("p b e -> p (b e)"), psL[:, 0:B * E]))
            flat = lambda a: a.rearrange("p b e f -> p b (e f)")
            mine = lg[:, :, :].unsqueeze(3).to_broadcast([P, B, E, E])
            other = lg[:, :, :].unsqueeze(2).to_broadcast([P, B, E, E])
            dve.tensor_tensor(gt[:, :, :, :], other, mine, ALU.is_gt).then_inc(route, 1)
            then(dve.tensor_tensor(eq[:, :, :, :], other, mine, ALU.is_equal))
            steps[0] += 1
            dve.wait_ge(route, steps[0])
            then(dve.tensor_tensor(flat(eql[:, :, :, :]), flat(eq[:, :, :, :]),
                                   lower[:, :, :].rearrange("p e f -> p (e f)").unsqueeze(1)
                                   .to_broadcast([P, B, E * E]), ALU.mult))
            then(dve.tensor_tensor(cnt[:, :, :, :], gt[:, :, :, :], eql[:, :, :, :], ALU.add))
            then(dve.tensor_reduce(rank[:, :, :], cnt[:, :, :, :], AX.X, ALU.add))
            dve.tensor_scalar(chosen[:, :, :], rank[:, :, :], TOPK - 0.5, None, ALU.is_lt).then_inc(choice_ready, 1)
            for k in range(TOPK):
                dve.tensor_scalar(sel[:, k, :, :], rank[:, :, :], float(k), None, ALU.is_equal)\
                   .then_inc(choice_ready, 1)
            dve.wait_ge(choice_ready, 3)
            for k in range(TOPK):
                dve.tensor_tensor(pick[:, 1, k, :, :], sel[:, k, :, :], lg[:, :, :], ALU.mult)\
                   .then_inc(choice_ready, 1)
            dve.wait_ge(count_done, 1)
            then(dve.tensor_copy(tot[:, :, :], psC[:, P:2 * P].rearrange("p (b e) -> p e b", e=E)))
            flat_tot = tot[:, :, :].rearrange("p e b -> p (e b)")
            then(dve.tensor_tensor_scan(scan[:, :], ones[:, :], flat_tot, 0.0, ALU.mult, ALU.add))
            then(dve.tensor_tensor(start[:, :, :].rearrange("p e b -> p (e b)"), scan[:, :], flat_tot, ALU.subtract))
            then(dve.tensor_tensor(pos[:, :, :], psC[:, 0:P].rearrange("p (b e) -> p b e", e=E),
                                   start[:, :, :].rearrange("p e b -> p b e"), ALU.add))
            for k in range(TOPK):
                dve.tensor_tensor(pick[:, 0, k, :, :], sel[:, k, :, :], pos[:, :, :], ALU.mult)\
                   .then_inc(choice_ready, 1)
            dve.wait_ge(choice_ready, 7)
            then(dve.tensor_reduce(picked[:, :, :, :].rearrange("p a k b -> p (a k) b"),
                                   pick[:, :, :, :, :].rearrange("p a k b e -> p (a k) b e"), AX.X, ALU.add))
            for k in range(TOPK):
                dve.tensor_copy(where[:, k, :], picked[:, 0, k, :]).then_inc(where_ready, 1)
            dve.tensor_tensor(dl[:, :], picked[:, 1, 1, :], picked[:, 1, 0, :], ALU.subtract).then_inc(dl_ready, 1)
            dve.wait_ge(ex_done, 1)
            then(dve.tensor_scalar(den[:, :], ex[:, :], 1.0, None, ALU.add))
            then(dve.reciprocal(wt[:, 0, :], den[:, :]))
            then(dve.tensor_tensor(wt[:, 1, :], wt[:, 0, :], ex[:, :], ALU.mult))

            with dve.Fori(0, E - 1, 2) as e0:
                for p in range(2):
                    e = e0 + p
                    dve.wait_ge(rT_done, e + 1)
                    dve.tensor_scalar(rowsT[:, :], psT[:, :, :].rearrange("p t n -> p (t n)"), 1.0, None, ALU.mult)\
                       .then_inc(rT_ready, 1)
                    dve.wait_ge(down_done, e + 1)
                    if p == 1:
                        dve.wait_ge(eo_out[1], e0 * 8)
                    dve.tensor_scalar(eo[:, p, :], psY[:, :], 1.0, None, ALU.mult).then_inc(eo_ready, 1)

            dve.wait_ge(gathered, 16 * TOPK * B)
            for k in range(TOPK):
                if k:
                    dve.wait_ge(x_step, B)
                for b in range(B):
                    dve.scalar_tensor_tensor(out=X[:, b, :], in0=got[:, k, b, :], scalar=wt[:, k, b:b + 1],
                                             in1=X[:, b, :], op0=ALU.mult, op1=ALU.add).then_inc(x_step, 1)
            dve.wait_ge(x_step, 2 * B)

        @block.scalar
        def _(act):
            for q in range(QUADS):
                act.wait_ge(t_done, q + 1)
                act.activation(xnT[:, q % 2, :, :], psT[:, :, :], ACT.Copy).then_inc(xnT_ready, 1)
            act.wait_ge(dl_ready, 1)
            act.activation(ex[:, :], dl[:, :], ACT.Exp).then_inc(ex_done, 1)
            with act.Fori(0, E - 1, 2) as e0:
                for p in range(2):
                    for f in range(FF // P):
                        act.wait_ge(up_done, e0 * 4 + 4 * p + f + 1)
                        act.activation(hid[:, p, f, :], psH[:, f, :], ACT.Gelu).then_inc(hid_ready, 1)

        @block.tensor
        def _(pe):
            pe.wait_ge(ld_c, 64)
            for q in range(QUADS):
                pe.wait_ge(xn_done, QUAD * q + QUAD)
                if q:
                    pe.wait_ge(xnT_ready, q)
                for t in range(QUAD):
                    mm = pe.transpose(psT[:, t, :], xn[:, QUAD * q + t, :], c.ident[:, :])
                mm.then_inc(t_done, 1)
                pe.wait_ge(xnT_ready, q + 1)
                for t in range(QUAD):
                    b = QUAD * q + t
                    pe.matmul(psL[:, E * b:E * b + E], xnT[:, q % 2, t, :], wrT[:, :], start=True, stop=True)\
                      .then_inc(lg_done, 1)
            pe.wait_ge(choice_ready, 3)
            ch = chosen[:, :, :].rearrange("p b e -> p (b e)")
            pe.matmul(psC[:, 0:P], before[:, :], ch, start=True, stop=True)
            pe.matmul(psC[:, P:2 * P], ones[:, :], ch, start=True, stop=True).then_inc(count_done, 1)

            def rows_in(e, p):
                pe.wait_ge(ld_r[p], e * 8 + 16 - 8 * p)
                for t in range(T4):
                    mm = pe.transpose(psT[:, t, :], rows[:, p, t, :], c.ident[:, :])
                mm.then_inc(rT_done, 1)

            def up(e, p):
                pe.wait_ge(ld_w[p], e * 16 + 32 - 16 * p)
                pe.wait_ge(rT_ready, e + 1)
                for f in range(FF // P):
                    pe.matmul(psH[:, f, :], w1[:, p, P * f:P * f + P], rowsT[:, :], start=True, stop=True)\
                      .then_inc(up_done, 1)

            def down(e, p, first):
                pe.wait_ge(hid_ready, e * 4 + 4)
                if not first:
                    pe.wait_ge(eo_ready, e)
                for t in range(T4):
                    for f in range(FF // P):
                        mm = pe.matmul(psY[:, D * t:D * t + D], hid[:, p, f, P * t:P * t + P], w2[:, p, f, :],
                                       start=(f == 0), stop=(f == FF // P - 1))
                mm.then_inc(down_done, 1)

            rows_in(0, 0)
            up(0, 0)
            rows_in(1, 1)
            down(0, 0, True)
            up(1, 1)
            with pe.Fori(2, E - 1, 2) as e0:
                for p in range(2):
                    rows_in(e0 + p, p)
                    down(e0 + p - 1, 1 - p, False)
                    up(e0 + p, p)
            down(E - 1, 1, False)


def second_attention(c):
    nc, io = c.nc, c.io
    with ExitStack() as ctx:
        sb = lambda name, shape, dt=F32: ctx.enter_context(nc.sbuf_tensor("c_" + name, shape, dt))
        ps = lambda name, shape, dt=F32: ctx.enter_context(nc.psum_tensor("c_" + name, shape, dt))
        sem = lambda name: c.sem("c_" + name)
        X = c.X
        ctx_in = sb("ctx_in", [P, B, D])
        xn = sb("xn", [P, B, D])
        w = sb("w", [P, 4, D])
        bqk = sb("bqk", [P, 2])
        bv = sb("bv", [P, D])
        bo = sb("bo", [P, D])
        xnT = sb("xnT", [P, QUAD, P])
        ctxT = sb("ctxT", [P, QUAD, P])
        qT = sb("qT", [P, QUAD, P])
        kT = sb("kT", [P, QUAD, P])
        v = sb("v", [P, 2, QUAD, D])
        mx = sb("mx", [P, QUAD])
        sd = sb("sd", [P, QUAD, P])
        pr = sb("pr", [P, 2, QUAD, P])
        den = sb("den", [P, QUAD])
        rden = sb("rden", [P, 2, QUAD])
        prT = sb("prT", [P, QUAD, P])
        att = sb("att", [P, QUAD, D])
        res = sb("res", [P, QUAD, D])
        resT = sb("resT", [P, QUAD, P])
        proj = sb("proj", [P, QUAD, D])

        psX, psC, psQ, psK, psV, psS, psB0, psB1 = (ps(n, [P, 4, P]) for n in
                                                    ("psX", "psC", "psQ", "psK", "psV", "psS", "psB0", "psB1"))
        ld = sem("ld")
        stats_done, ln_step, rstd_done, xn_done = sem("stats_done"), sem("ln_step"), sem("rstd_done"), sem("xn_done")
        tx_done, tc_done, xnT_ready, ctxT_ready = sem("tx_done"), sem("tc_done"), sem("xnT_ready"), sem("ctxT_ready")
        q_done, k_done, v_done = sem("q_done"), sem("k_done"), sem("v_done")
        q_ready, k_ready, v_ready = sem("q_ready"), sem("k_ready"), sem("v_ready")
        s_done, mx_done, sd_done, exp_done = sem("s_done"), sem("mx_done"), sem("sd_done"), sem("exp_done")
        den_done, rden_done, pT_done, pT_ready = sem("den_done"), sem("rden_done"), sem("pT_done"), sem("pT_ready")
        a_done, att_done, res_done = sem("a_done"), sem("att_done"), sem("res_done")
        rT_done, rT_ready, o_done, proj_done, x_done = (sem("rT_done"), sem("rT_ready"), sem("o_done"),
                                                        sem("proj_done"), sem("x_done"))
        block = ctx.enter_context(nc.Block())

        @block.sync
        def _(sp):
            sp.dma_start(ctx_in[:, :, :], io["ctx_1024"].rearrange("b t d -> t b d")).then_inc(ld, 16)
            sp.dma_start(w[:, :, :], io["l_w1x"]).then_inc(ld, 16)
            sp.dma_start(bqk[:, :], io["l_b1x"]).then_inc(ld, 16)
            sp.dma_start(bv[:, :], io["L1_xattn_bv"].partition_broadcast(P)).then_inc(ld, 16)
            sp.dma_start(bo[:, :], io["L1_xattn_bo"].partition_broadcast(P)).then_inc(ld, 16)

        @block.gpsimd
        def _(pool):
            ln_rstd_pool(pool, c, ln_step, rstd_done)

        @block.vector
        def _(dve):
            ln_stats_dve(dve, c, stats_done, ln_step, X)
            dve.wait_ge(rstd_done, 2)
            for b in range(B):
                dve.tensor_scalar(xn[:, b, :], X[:, b, :], c.meanvar[:, b, 0:1], c.rstd[:, b:b + 1],
                                  ALU.subtract, ALU.mult).then_inc(xn_done, 1)
            dve.wait_ge(ld, 80)

            def front(q):
                dve.wait_ge(tc_done, q + 1)
                dve.tensor_copy(ctxT[:, :, :], psC[:, :, :]).then_inc(ctxT_ready, 1)
                dve.wait_ge(q_done, q + 1)
                dve.tensor_scalar(qT[:, :, :], psQ[:, :, :], bqk[:, 0:1], None, ALU.add).then_inc(q_ready, 1)
                dve.wait_ge(v_done, q + 1)
                dve.tensor_tensor(v[:, q % 2, :, :], psV[:, :, :], bv[:, :].unsqueeze(1).to_broadcast([P, QUAD, D]),
                                  ALU.add).then_inc(v_ready, 1)
                dve.wait_ge(s_done, q + 1)
                dve.tensor_reduce(mx[:, :], psS[:, :, :], AX.X, ALU.max).then_inc(mx_done, 1)
                dve.wait_ge(mx_done, q + 1)
                dve.tensor_tensor(sd[:, :, :], psS[:, :, :], mx[:, :].unsqueeze(2).to_broadcast([P, QUAD, P]),
                                  ALU.subtract).then_inc(sd_done, 1)
                dve.wait_ge(exp_done, q + 1)
                dve.tensor_reduce(den[:, :], pr[:, q % 2, :, :], AX.X, ALU.add).then_inc(den_done, 1)
                dve.wait_ge(den_done, q + 1)
                dve.reciprocal(rden[:, q % 2, :], den[:, :]).then_inc(rden_done, 1)

            def back(q):
                dve.wait_ge(a_done, q + 1)
                dve.wait_ge(rden_done, q + 1)
                dve.tensor_tensor(att[:, :, :], psB1[:, :, :], rden[:, q % 2, :].unsqueeze(2)
                                  .to_broadcast([P, QUAD, D]), ALU.mult).then_inc(att_done, 1)
                dve.wait_ge(att_done, q + 1)
                dve.tensor_tensor(res[:, :, :], att[:, :, :], xn[:, QUAD * q:QUAD * q + QUAD, :], ALU.add)\
                   .then_inc(res_done, 1)
                dve.wait_ge(o_done, q + 1)
                dve.tensor_tensor(proj[:, :, :], psB1[:, :, :], bo[:, :].unsqueeze(1).to_broadcast([P, QUAD, D]),
                                  ALU.add).then_inc(proj_done, 1)
                dve.wait_ge(proj_done, q + 1)
                xq = X[:, QUAD * q:QUAD * q + QUAD, :]
                dve.tensor_tensor(xq, proj[:, :, :], xq, ALU.add).then_inc(x_done, 1)

            front(0)
            for q in range(QUADS):
                if q + 1 < QUADS:
                    front(q + 1)
                back(q)
            dve.wait_ge(x_done, QUADS)

        @block.scalar
        def _(act):
            act.wait_ge(ld, 80)

            def front(q):
                act.wait_ge(tx_done, q + 1)
                act.activation(xnT[:, :, :], psX[:, :, :], ACT.Copy).then_inc(xnT_ready, 1)
                act.wait_ge(k_done, q + 1)
                act.activation(kT[:, :, :], psK[:, :, :], ACT.Identity, bias=bqk[:, 1:2]).then_inc(k_ready, 1)
                act.wait_ge(sd_done, q + 1)
                act.activation(pr[:, q % 2, :, :], sd[:, :, :], ACT.Exp, scale=SCALE1).then_inc(exp_done, 1)

            def back(q):
                act.wait_ge(pT_done, q + 1)
                act.activation(prT[:, :, :], psB0[:, :, :], ACT.Copy).then_inc(pT_ready, 1)
                act.wait_ge(rT_done, q + 1)
                act.activation(resT[:, :, :], psB0[:, :, :], ACT.Copy).then_inc(rT_ready, 1)

            front(0)
            for q in range(QUADS):
                if q + 1 < QUADS:
                    front(q + 1)
                back(q)

        @block.tensor
        def _(pe):
            pe.wait_ge(ld, 80)

            def front(q):
                pe.wait_ge(xn_done, QUAD * q + QUAD)
                if q:
                    pe.wait_ge(sd_done, q)
                for t in range(QUAD):
                    mm = pe.transpose(psX[:, t, :], xn[:, QUAD * q + t, :], c.ident[:, :])
                mm.then_inc(tx_done, 1)
                for t in range(QUAD):
                    mm = pe.transpose(psC[:, t, :], ctx_in[:, QUAD * q + t, :], c.ident[:, :])
                mm.then_inc(tc_done, 1)
                pe.wait_ge(xnT_ready, q + 1)
                pe.matmul(psQ[:, :, :].rearrange("p t n -> p (t n)"), w[:, 0, :],
                          xnT[:, :, :].rearrange("p t n -> p (t n)"), start=True, stop=True).then_inc(q_done, 1)
                pe.wait_ge(ctxT_ready, q + 1)
                pe.matmul(psK[:, :, :].rearrange("p t n -> p (t n)"), w[:, 1, :],
                          ctxT[:, :, :].rearrange("p t n -> p (t n)"), start=True, stop=True).then_inc(k_done, 1)
                for t in range(QUAD):
                    mm = pe.matmul(psV[:, t, :], ctxT[:, t, :], w[:, 2, :], start=True, stop=True)
                mm.then_inc(v_done, 1)
                pe.wait_ge(q_ready, q + 1)
                pe.wait_ge(k_ready, q + 1)
                for t in range(QUAD):
                    mm = pe.matmul(psS[:, t, :], qT[:, t, :], kT[:, t, :], start=True, stop=True)
                mm.then_inc(s_done, 1)

            def back(q):
                pe.wait_ge(exp_done, q + 1)
                if q:
                    pe.wait_ge(rT_ready, q)
                for t in range(QUAD):
                    mm = pe.transpose(psB0[:, t, :], pr[:, q % 2, t, :], c.ident[:, :])
                mm.then_inc(pT_done, 1)
                pe.wait_ge(pT_ready, q + 1)
                pe.wait_ge(v_ready, q + 1)
                if q:
                    pe.wait_ge(proj_done, q)
                for t in range(QUAD):
                    mm = pe.matmul(psB1[:, t, :], prT[:, t, :], v[:, q % 2, t, :], start=True, stop=True)
                mm.then_inc(a_done, 1)
                pe.wait_ge(res_done, q + 1)
                for t in range(QUAD):
                    mm = pe.transpose(psB0[:, t, :], res[:, t, :], c.ident[:, :])
                mm.then_inc(rT_done, 1)
                pe.wait_ge(rT_ready, q + 1)
                for t in range(QUAD):
                    mm = pe.matmul(psB1[:, t, :], resT[:, t, :], w[:, 3, :], start=True, stop=True)
                mm.then_inc(o_done, 1)

            front(0)
            for q in range(QUADS):
                if q + 1 < QUADS:
                    front(q + 1)
                back(q)


def local_transformer(c):
    nc, io = c.nc, c.io
    with ExitStack() as ctx:
        sb = lambda name, shape, dt=F32: ctx.enter_context(nc.sbuf_tensor("d_" + name, shape, dt))
        ps = lambda name, shape, dt=F32: ctx.enter_context(nc.psum_tensor("d_" + name, shape, dt))
        sem = lambda name: c.sem("d_" + name)
        X = c.X
        KEYS = 2 * WINDOW
        WINDOWS = P // WINDOW
        HALF = D // 2

        Y = sb("Y", [P, B, D])
        w_qkv = sb("w_qkv", [P, 3 * INNER])
        w_o = sb("w_o", [P, INNER // P, D])
        w1 = sb("w1", [P, 6, P])
        w2 = sb("w2", [P, 3, D])
        cols = sb("cols", [P, 8])
        b2 = sb("b2", [P, D])
        scales = sb("scales", [P, LAYERS, 2, DH])
        rot = sb("rot", [P, 4, DH])
        tab = sb("tab", [P, 4, DH])
        mask_in = sb("mask_in", [P, KEYS])
        mask = sb("mask", [P, 4 * KEYS], BF16)
        ident_bf = sb("ident_bf", [P, P], BF16)
        shift = sb("shift", [P, P])

        y_in = sb("y_in", [P, D])
        xsT = sb("xsT", [P, P])
        sq = sb("sq", [P, 2 * UH, DH])
        ss = sb("ss", [P, 2, 2 * UH])
        rn = sb("rn", [P, 2, 2 * UH])
        mhalf = sb("mhalf", [P, 2 * UH])
        raw = sb("raw", [P, 2, 2 * UH, DH])
        tc = sb("tc", [P, 2, 2 * UH, DH])
        ts = sb("ts", [P, 2, 2 * UH, DH])
        rs = sb("rs", [P, 2 * UH, DH])
        qr = sb("qr", [P, 2, 2 * UH * DH])
        qT = sb("qT", [P, 4, P])
        kT = sb("kT", [P, 4, WINDOW + P])
        v1 = sb("v1", [P, 4, UH, DH])
        mx = sb("mx", [P, 2, 4])
        sd = sb("sd", [P, 2, 2, 4, KEYS])
        pr = sb("pr", [P, 2, 2, 4, P])
        prT = sb("prT", [P, 2, 4, P])
        den = sb("den", [P, UH])
        rden = sb("rden", [P, UH])
        oT = sb("oT", [P, INNER // P, P])

        xs = sb("xs", [P, 2, QUAD, D])
        xn = sb("xn", [P, 2, QUAD, D])
        xnT = sb("xnT", [P, QUAD * P])
        gate = sb("gate", [P, 2, QUAD * P])
        hid = sb("hid", [P, 3, QUAD * P])
        yb = sb("yb", [P, QUAD, D])
        fstats = sb("fstats", [P, QUAD, 6])
        fmv = sb("fmv", [P, QUAD, 2])
        fve = sb("fve", [P, QUAD])
        frs = sb("frs", [P, QUAD])

        psQK = ps("psQK", [P, 2, BANK])
        psV = ps("psV", [P, BANK])
        psT0 = ps("psT0", [P, 4, P])
        psT1 = ps("psT1", [P, 4, P])
        psS = ps("psS", [P, 2, BANK])
        psM = ps("psM", [P, BANK])
        tin = psT0[:, 0, :]
        scores = psS[:, :, 0:4 * KEYS].rearrange("p r (c k) -> p r c k", c=4)
        pair = [psQK, psS]

        ld_c, ld_attn, ld_ffn = sem("ld_c"), sem("ld_attn"), sem("ld_ffn")
        stats_done, ln_step, rstd_done = sem("stats_done"), sem("ln_step"), sem("rstd_done")
        zeroed, tab_done, tab_ready = sem("zeroed"), sem("tab_done"), sem("tab_ready")
        layer_in, attn_out = sem("layer_in"), sem("attn_out")
        yin_ready, t_done, xs_ready = sem("yin_ready"), sem("t_done"), sem("xs_ready")
        qk_proj, v_proj, v_ready = sem("qk_proj"), sem("v_proj"), sem("v_ready")
        sq_done, ss_done, rn_done = sem("sq_done"), sem("ss_done"), sem("rn_done")
        raw_done, tc_done, ts_done = sem("raw_done"), sem("tc_done"), sem("ts_done")
        rs_done, qr_done = sem("rs_done"), sem("qr_done")
        qT_done, qT_ready, kT_done, kT_ready = sem("qT_done"), sem("qT_ready"), sem("kT_done"), sem("kT_ready")
        s_done, mx_done, sd_done, exp_done = sem("s_done"), sem("mx_done"), sem("sd_done"), sem("exp_done")
        pT0_done, pT0_ready = sem("pT0_done"), sem("pT0_ready")
        pT1_done, pT1_ready = sem("pT1_done"), sem("pT1_ready")
        den_done, rden_done, norm_done, pr_done = sem("den_done"), sem("rden_done"), sem("norm_done"), sem("pr_done")
        pv_done, oT_ready, wo_done = sem("pv_done"), sem("oT_ready"), sem("wo_done")
        sh_done, fxs_ready, fstat, fve_done = sem("sh_done"), sem("fxs_ready"), sem("fstat"), sem("fve_done")
        frs_done, fxn_done, fT_done, fT_ready = sem("frs_done"), sem("fxn_done"), sem("fT_done"), sem("fT_ready")
        up_done, gate_done, hid_done = sem("up_done"), sem("gate_done"), sem("hid_done")
        down_done, yb_done, x_done = sem("down_done"), sem("yb_done"), sem("x_done")

        block = ctx.enter_context(nc.Block())

        @block.sync
        def _(sp):
            for dst, name in ((rot, "c_rot"), (mask_in, "c_mask"), (shift, "c_shift")):
                sp.dma_start(dst[:], io[name]).then_inc(ld_c, 16)
            sp.dma_start(scales[:, :, :, :], io["l_scales"].partition_broadcast(P)).then_inc(ld_c, 16)

            def load_attn(l):
                sp.dma_start(w_qkv[:, :], io["L1_ffn_Wqkv"][one(l), :, :].rearrange("o k n -> k (o n)"))\
                  .then_inc(ld_attn, 16)
                sp.dma_start(w_o[:, :, :], io["L1_ffn_Wo"][one(l), :, :].rearrange("o (c k) n -> k (o c) n", k=P))\
                  .then_inc(ld_attn, 16)

            def load_ffn(l):
                sp.dma_start(w1[:, :, :], io["l_w1"][one(l), :, :, :].rearrange("o k c n -> k (o c) n"))\
                  .then_inc(ld_ffn, 16)
                sp.dma_start(w2[:, :, :], io["l_w2"][one(l), :, :, :].rearrange("o k c n -> k (o c) n"))\
                  .then_inc(ld_ffn, 16)
                sp.dma_start(cols[:, :], io["l_cols"][one(l), :, :].rearrange("o k n -> k (o n)")).then_inc(ld_ffn, 16)
                sp.dma_start(b2[:, :], io["L1_ffn_b2"][one(l), :].rearrange("o n -> (o n)").partition_broadcast(P))\
                  .then_inc(ld_ffn, 16)

            load_attn(0)
            load_ffn(0)
            with sp.Fori(1, LAYERS) as l:
                sp.wait_ge(wo_done, l * B)
                load_attn(l)
                sp.wait_ge(layer_in, l * B + B)
                load_ffn(l)

        @block.gpsimd
        def _(pool):
            pool.memset(kT[:, :, 0:WINDOW], 0.0).then_inc(zeroed, 1)
            pool.memset(pr[:, :, :, :, :], 0.0).then_inc(zeroed, 1)
            pool.memset(mhalf[:, :], -0.5).then_inc(zeroed, 1)
            ln_rstd_pool(pool, c, ln_step, rstd_done)
            pool.wait_ge(ld_c, 16 * 4)
            pool.wait_ge(zeroed, 6)
            with pool.Fori(0, LAYERS) as l:
                batches, steps, quads = l * B, l * UNITS, l * QUADS

                sc = scales[:, one(l), :, :].rearrange("p o a d -> p (o a) d")
                pool.tensor_tensor(tab[:, 0:2, :], rot[:, 0:2, :], sc, ALU.mult).then_inc(tab_done, 1)
                for to, frm in ((0, DH // 2), (DH // 2, 0)):
                    pool.tensor_tensor(tab[:, 2:4, to:to + DH // 2], rot[:, 2:4, to:to + DH // 2],
                                       sc[:, :, frm:frm + DH // 2], ALU.mult).then_inc(tab_done, 1)
                pool.wait_ge(tab_done, l * 3 + 3)

                def body(b, i, s, live):
                    u = s % 2
                    if live(0):
                        pool.wait_ge(raw_done, steps + i + 1)
                        for to, frm in ((0, DH // 2), (DH // 2, 0)):
                            t = tab[:, 2:4, to:to + DH // 2].unsqueeze(2).to_broadcast([P, 2, UH, DH // 2])
                            pool.tensor_tensor(
                                ts[:, u, :, to:to + DH // 2].rearrange("p (a h) d -> p a h d", a=2),
                                raw[:, u, :, frm:frm + DH // 2].rearrange("p (a h) d -> p a h d", a=2),
                                t, ALU.mult).then_inc(ts_done, 1)
                        pool.wait_ge(ss_done, steps + i + 1)
                        pool.tensor_tensor(rn[:, u, :], ss[:, u, :], mhalf[:, :], ALU.pow).then_inc(rn_done, 1)

                units(pool, body, 0)
                pool.wait_ge(ld_ffn, l * 64 + 64)
                pool.wait_ge(attn_out, batches + B + 1)
                for q in range(QUADS):
                    pool.wait_ge(fve_done, quads + q + 1)
                    pool.tensor_tensor(frs[:, :], fve[:, :], mhalf[:, 0:QUAD], ALU.pow).then_inc(frs_done, 1)
                    if q >= 1:
                        pool.wait_ge(layer_in, batches + B + QUAD * q)
                    pool.tensor_tensor(yb[:, :, :], Y[:, QUAD * q:QUAD * q + QUAD, :],
                                       b2[:, :].unsqueeze(1).to_broadcast([P, QUAD, D]), ALU.add)\
                        .then_inc(yb_done, 1)

        @block.vector
        def _(dve):
            dve.memset(xsT[HALF:, 0:1], 0.0).then_inc(zeroed, 1)
            dve.memset(den[:, :], 1.0).then_inc(attn_out, 1)
            dve.wait_ge(ld_c, 16 * 4)
            dve.tensor_copy(mask[:, :].rearrange("p (c k) -> p c k", c=4),
                            mask_in[:, :].unsqueeze(1).to_broadcast([P, 4, KEYS])).then_inc(zeroed, 1)
            dve.tensor_copy(ident_bf[:, :], c.ident[:, :]).then_inc(zeroed, 1)
            ln_stats_dve(dve, c, stats_done, ln_step, X)
            dve.wait_ge(rstd_done, 2)
            for b in range(B):
                dve.tensor_scalar(Y[:, b, :], X[:, b, :], c.meanvar[:, b, 0:1], c.rstd[:, b:b + 1],
                                  ALU.subtract, ALU.mult).then_inc(layer_in, 1)
            dve.wait_ge(zeroed, 6)
            with dve.Fori(0, LAYERS) as l:
                batches, steps, quads = l * B, l * UNITS, l * QUADS

                def stage(b):
                    dve.tensor_scalar(y_in[:, :], row(Y[:, one(b), :]), 1.0, None, ALU.mult).then_inc(yin_ready, 1)

                dve.wait_ge(layer_in, batches + B)
                stage(0)
                dve.wait_ge(tab_done, l * 3 + 3)

                def rotated(j, t):
                    dve.wait_ge(rs_done, steps + j + 1)
                    dve.wait_ge(rn_done, steps + j + 1)
                    dve.scalar_tensor_tensor(out=qr[:, t, :].rearrange("p (h d) -> p h d", d=DH),
                                             in0=rn[:, t, :].unsqueeze(2).to_broadcast([P, 2 * UH, DH]),
                                             scalar=1e12, in1=rs[:, :, :],
                                             op0=ALU.min, op1=ALU.mult).then_inc(qr_done, 1)

                def body(b, i, s, live):
                    u = s % 2
                    if live(1):
                        rotated(i - 1, 1 - u)
                    if live(2):
                        dve.wait_ge(exp_done, steps + i - 1)
                        dve.tensor_reduce(den[:, :], sd[:, u, :, :, :].rearrange("p r c k -> p (r c) k"),
                                          AX.X, ALU.add).then_inc(den_done, 1)
                        dve.wait_ge(den_done, steps + i - 1)
                        dve.reciprocal(rden[:, :], den[:, :]).then_inc(rden_done, 1)
                        dve.wait_ge(rden_done, steps + i - 1)
                        e = sd[:, u, :, :, :].rearrange("p r c k -> p (r c) k")
                        dve.tensor_tensor(e, e, rden[:, :].unsqueeze(2).to_broadcast([P, UH, KEYS]), ALU.mult)\
                           .then_inc(norm_done, 1)
                    if live(0):
                        if u == 1 and live(-1):
                            dve.wait_ge(t_done, batches + b + 1)
                            stage(b + 1)
                        dve.wait_ge(raw_done, steps + i + 1)
                        dve.tensor_tensor(tc[:, u, :, :].rearrange("p (a h) d -> p a h d", a=2),
                                          raw[:, u, :, :].rearrange("p (a h) d -> p a h d", a=2),
                                          tab[:, 0:2, :].unsqueeze(2).to_broadcast([P, 2, UH, DH]),
                                          ALU.mult).then_inc(tc_done, 1)
                        dve.wait_ge(sq_done, steps + i + 1)
                        dve.tensor_reduce(ss[:, u, :], sq[:, :, :], AX.X, ALU.add).then_inc(ss_done, 1)
                    if live(4) and u == 1:
                        dve.wait_ge(wo_done, batches + b - 1)
                        dve.tensor_tensor(row(Y[:, one(b - 2), :]), psM[:, 0:D], row(Y[:, one(b - 2), :]),
                                          ALU.add).then_inc(attn_out, 1)
                    if live(0):
                        dve.wait_ge(tc_done, steps + i + 1)
                        dve.wait_ge(ts_done, steps * 2 + i * 2 + 2)
                        dve.tensor_tensor(rs[:, :, :].rearrange("p h d -> p (h d)"),
                                          tc[:, u, :, :].rearrange("p h d -> p (h d)"),
                                          ts[:, u, :, :].rearrange("p h d -> p (h d)"), ALU.add).then_inc(rs_done, 1)
                    if live(1):
                        v = (s - 1) % 2
                        dve.wait_ge(s_done, steps + i)
                        dve.tensor_reduce(mx[:, :, :], scores, AX.X, ALU.max).then_inc(mx_done, 1)
                        dve.wait_ge(mx_done, steps + i)
                        if live(3):
                            dve.wait_ge(pr_done, steps * 4 + i * 4 - 8)
                        dve.tensor_tensor(sd[:, v, :, :, :], scores,
                                          mx[:, :, :].unsqueeze(3).to_broadcast([P, 2, 4, KEYS]),
                                          ALU.subtract).then_inc(sd_done, 1)

                units(dve, body, 4)

                dve.wait_ge(ld_ffn, l * 64 + 64)

                def normalize(q):
                    v = q % 2
                    dve.wait_ge(fxs_ready, quads * 2 + 2 * q + 2)
                    for t in range(QUAD):
                        dve.bn_stats(fstats[:, t, :], xs[:, v, t, :]).then_inc(fstat, 1)
                    dve.wait_ge(fstat, quads * 8 + 8 * q + 4)
                    dve.memset(fve[:, :], 0.0)
                    for t in range(QUAD):
                        dve.bn_aggr(fmv[:, t, :], fstats[:, t, :]).then_inc(fstat, 1)
                    dve.wait_ge(fstat, quads * 8 + 8 * q + 8)
                    dve.tensor_scalar(fve[:, :], fmv[:, :, 1], LN_EPS, None, ALU.add).then_inc(fve_done, 1)
                    dve.wait_ge(frs_done, quads + q + 1)
                    for t in range(QUAD):
                        dve.tensor_scalar(xn[:, v, t, :], xs[:, v, t, :], fmv[:, t, 0:1], frs[:, t:t + 1],
                                          ALU.subtract, ALU.mult).then_inc(fxn_done, 1)

                normalize(0)
                for q in range(QUADS):
                    dve.wait_ge(fT_done, quads + q + 1)
                    dve.tensor_scalar(xnT[:, :], psT0[:, :, :].rearrange("p t n -> p (t n)"), cols[:, 6:7],
                                      cols[:, 7:8], ALU.mult, ALU.add).then_inc(fT_ready, 1)
                    if q + 1 < QUADS:
                        normalize(q + 1)
                    for ch in range(3):
                        v = (3 * q + ch) % 2
                        dve.wait_ge(gate_done, quads * 3 + 3 * q + ch + 1)
                        dve.scalar_tensor_tensor(out=hid[:, ch, :], in0=pair[v][:, 0, :], scalar=cols[:, ch:ch + 1],
                                                 in1=gate[:, v, :], op0=ALU.add, op1=ALU.mult)\
                           .then_inc(hid_done, 1)
                    dve.wait_ge(down_done, quads + q + 1)
                    dve.wait_ge(yb_done, quads + q + 1)
                    dve.tensor_tensor(Y[:, QUAD * q:QUAD * q + QUAD, :].rearrange("p t n -> p (t n)"), psM[:, :],
                                      yb[:, :, :].rearrange("p t n -> p (t n)"), ALU.add)\
                       .then_inc(layer_in, QUAD)

            dve.wait_ge(layer_in, B + LAYERS * B)
            dve.tensor_tensor(X[:, :, :], X[:, :, :], Y[:, :, :], ALU.add).then_inc(x_done, 1)
            dve.wait_ge(x_done, 1)

        @block.scalar
        def _(act):
            act.wait_ge(zeroed, 6)
            with act.Fori(0, LAYERS) as l:
                batches, steps, quads = l * B, l * UNITS, l * QUADS

                def evac_x(b):
                    act.wait_ge(t_done, batches + b + 1)
                    act.activation(xsT[0:HALF, :], tin[0:HALF, :], ACT.Copy).then_inc(xs_ready, 1)
                    act.activation(xsT[HALF:, 1:P], tin[HALF:, 0:P - 1], ACT.Copy).then_inc(xs_ready, 1)

                evac_x(0)

                def body(b, i, s, live):
                    u = s % 2
                    if live(2):
                        act.wait_ge(sd_done, steps + i - 1)
                        e = sd[:, u, :, :, :].rearrange("p r c k -> p (r c k)")
                        act.activation(e, e, ACT.Exp).then_inc(exp_done, 1)
                    if live(0):
                        act.wait_ge(qk_proj, steps + i + 1)
                        if live(2):
                            act.wait_ge(rs_done, steps + i - 1)
                        act.activation(raw[:, u, :, :], psQK[:, :, :].rearrange("p a (h d) -> p (a h) d", h=UH),
                                       ACT.Copy).then_inc(raw_done, 1)
                    if live(3):
                        act.wait_ge(pT1_done, steps + i - 2)
                        act.activation(prT[:, 0, :, :], psT1[:, :, :], ACT.Copy).then_inc(pT1_ready, 1)
                        act.wait_ge(pT0_done, steps + i - 2)
                        act.activation(prT[:, 1, :, :], psT0[:, :, :], ACT.Copy).then_inc(pT0_ready, 1)
                    if live(0):
                        act.wait_ge(v_proj, steps + i + 1)
                        act.activation(v1[:, s, :, :], psV[:, :].rearrange("p (n d) -> p n d", d=DH),
                                       ACT.Copy).then_inc(v_ready, 1)
                        if live(1):
                            act.wait_ge(ss_done, steps + i)
                        act.activation(sq[:, :, :], psQK[:, :, :].rearrange("p a (h d) -> p (a h) d", h=UH),
                                       ACT.Square).then_inc(sq_done, 1)
                    if live(1):
                        act.wait_ge(kT_done, steps + i)
                        act.activation(kT[:, :, WINDOW:], psT1[:, :, :], ACT.Copy).then_inc(kT_ready, 1)
                        act.wait_ge(qT_done, steps + i)
                        act.activation(qT[:, :, :], psT0[:, :, :], ACT.Copy).then_inc(qT_ready, 1)
                    if live(3):
                        act.wait_ge(pv_done, steps + i - 2)
                        w = (s - 3) % 2
                        act.activation(oT[:, 4 * w:4 * w + 4, :].rearrange("p c q -> p (c q)"), psV[:, :], ACT.Copy)\
                           .then_inc(oT_ready, 1)
                    if live(0) and u == 1 and live(-1):
                        evac_x(b + 1)
                    if live(2):
                        act.wait_ge(norm_done, steps + i - 1)
                        for w in range(WINDOWS):
                            r, lo = slice(WINDOW * w, WINDOW * w + WINDOW), max(0, WINDOW * (w - 1))
                            hi = WINDOW * (w + 1)
                            act.activation(pr[r, u, :, :, lo:hi].rearrange("p r c k -> p (r c) k"),
                                           sd[r, u, :, :, KEYS - (hi - lo):].rearrange("p r c k -> p (r c) k"),
                                           ACT.Copy).then_inc(pr_done, 1)

                units(act, body, 3)

                def shifted(q):
                    v = q % 2
                    act.wait_ge(attn_out, batches + B + 1)
                    if q >= 2:
                        act.wait_ge(fxn_done, batches + QUAD * (q - 1))
                    act.activation(xs[:, v, :, 0:HALF], Y[:, QUAD * q:QUAD * q + QUAD, 0:HALF], ACT.Copy)\
                       .then_inc(fxs_ready, 1)
                    act.wait_ge(sh_done, quads + q + 1)
                    act.activation(xs[:, v, :, HALF:], psV[:, 0:QUAD * HALF].rearrange("p (t n) -> p t n", t=QUAD),
                                   ACT.Copy).then_inc(fxs_ready, 1)

                act.wait_ge(ld_ffn, l * 64 + 64)
                shifted(0)
                for q in range(QUADS):
                    if q + 1 < QUADS:
                        shifted(q + 1)
                    for ch in range(3):
                        n = 3 * q + ch
                        act.wait_ge(up_done, quads * 3 + n + 1)
                        if n >= 2:
                            act.wait_ge(hid_done, quads * 3 + n - 1)
                        act.activation(gate[:, n % 2, :], pair[n % 2][:, 1, :], ACT.Gelu, bias=cols[:, 3 + ch:4 + ch])\
                           .then_inc(gate_done, 1)

        @block.tensor
        def _(pe):
            pe.wait_ge(ld_c, 16 * 4)
            pe.wait_ge(zeroed, 6)
            with pe.Fori(0, LAYERS) as l:
                batches, steps, quads = l * B, l * UNITS, l * QUADS

                def transpose_in(b):
                    pe.wait_ge(yin_ready, batches + b + 1)
                    pe.transpose(tin, y_in[:, :], c.ident[:, :]).then_inc(t_done, 1)

                transpose_in(0)
                pe.wait_ge(ld_attn, l * 32 + 32)

                def body(b, i, s, live):
                    u = s % 2
                    if live(0):
                        pe.wait_ge(xs_ready, batches * 2 + b * 2 + 2)
                        if live(1):
                            pe.wait_ge(sq_done, steps + i)
                        for qk in range(2):
                            at = INNER * qk + UH * DH * u
                            mm = pe.matmul(psQK[:, qk, :], xsT[:, :], w_qkv[:, at:at + UH * DH],
                                           start=True, stop=True)
                        mm.then_inc(qk_proj, 1)
                    if live(3):
                        v = (s - 3) % 2
                        pe.wait_ge(pr_done, steps * 4 + i * 4 - 8)
                        for ch in range(4):
                            mm = pe.transpose(psT1[:, ch, :], pr[:, v, 0, ch, :], c.ident[:, :])
                        mm.then_inc(pT1_done, 1)
                        for ch in range(4):
                            mm = pe.transpose(psT0[:, ch, :], pr[:, v, 1, ch, :], c.ident[:, :])
                        mm.then_inc(pT0_done, 1)
                    if live(0):
                        if live(4):
                            pe.wait_ge(oT_ready, steps + i - 3)
                        elif live(1):
                            pe.wait_ge(v_ready, steps + i)
                        at = 2 * INNER + UH * DH * u
                        pe.matmul(psV[:, :], xsT[:, :], w_qkv[:, at:at + UH * DH], start=True, stop=True)\
                          .then_inc(v_proj, 1)
                    if live(4):
                        pe.wait_ge(oT_ready, steps + i - 3)
                        if u == 0:
                            pe.wait_ge(attn_out, batches + b - 1)
                        for ch in range(4):
                            mm = pe.matmul(psM[:, 0:D], oT[:, 4 * u + ch, :], w_o[:, 4 * u + ch, :],
                                           start=(u == 0 and ch == 0), stop=(u == 1 and ch == 3))
                        if u == 1:
                            mm.then_inc(wo_done, 1)
                    if live(1):
                        v = (s - 1) % 2
                        pe.wait_ge(qr_done, steps + i)
                        if live(3):
                            pe.wait_ge(pT1_ready, steps + i - 2)
                        for ch in range(4):
                            mm = pe.transpose(psT1[:, ch, :], qr[:, v, 512 + P * ch:512 + P * ch + P], c.ident[:, :])
                        mm.then_inc(kT_done, 1)
                        if live(3):
                            pe.wait_ge(pT0_ready, steps + i - 2)
                        for ch in range(4):
                            mm = pe.transpose(psT0[:, ch, :], qr[:, v, P * ch:P * ch + P], c.ident[:, :])
                        mm.then_inc(qT_done, 1)
                    if live(3):
                        q = (s - 3) % 4
                        pe.wait_ge(pT0_ready, steps + i - 2)
                        pe.wait_ge(pT1_ready, steps + i - 2)
                        if live(0):
                            pe.wait_ge(v_ready, steps + i + 1)
                        if live(4):
                            pe.wait_ge(oT_ready, steps + i - 3)
                        for ch in range(4):
                            for r in range(2):
                                mm = pe.matmul(psV[DH * r:DH * r + DH, P * ch:P * ch + P], v1[:, q, 2 * ch + r, :],
                                               prT[:, r, ch, :], start=True, stop=True)
                        mm.then_inc(pv_done, 1)
                    if live(0) and u == 1 and live(-1):
                        pe.wait_ge(qT_ready, steps + i)
                        transpose_in(b + 1)
                    if live(1):
                        pe.wait_ge(kT_ready, steps + i)
                        pe.wait_ge(qT_ready, steps + i)
                        if live(2):
                            pe.wait_ge(sd_done, steps + i - 1)
                        for r in range(2):
                            pe.matmul(psS[:, r, 0:4 * KEYS], ident_bf[:, :], mask[:, :], start=True, stop=False,
                                      skip_group_check=True)
                        for ch in range(4):
                            for r in range(2):
                                rows = slice(DH * r, DH * r + DH)
                                for w in range(WINDOWS):
                                    mm = pe.matmul(psS[WINDOW * w:WINDOW * w + WINDOW, r, KEYS * ch:KEYS * ch + KEYS],
                                                   qT[rows, ch, WINDOW * w:WINDOW * w + WINDOW],
                                                   kT[rows, ch, WINDOW * w:WINDOW * w + KEYS],
                                                   start=False, stop=True, skip_group_check=True)
                        mm.then_inc(s_done, 1)
                units(pe, body, 4)

                pe.wait_ge(attn_out, batches + B + 1)
                pe.wait_ge(ld_ffn, l * 64 + 64)

                def shift_tokens(q):
                    if q >= 1:
                        pe.wait_ge(fxs_ready, quads * 2 + 2 * q)
                    pe.matmul(psV[:, 0:QUAD * HALF], shift[:, :], Y[:, QUAD * q:QUAD * q + QUAD, HALF:],
                              start=True, stop=True).then_inc(sh_done, 1)

                shift_tokens(0)
                for q in range(QUADS):
                    if q + 1 < QUADS:
                        shift_tokens(q + 1)
                    pe.wait_ge(fxn_done, batches + QUAD * q + QUAD)
                    for t in range(QUAD):
                        mm = pe.transpose(psT0[:, t, :], xn[:, q % 2, t, :], c.ident[:, :])
                    mm.then_inc(fT_done, 1)
                    pe.wait_ge(fT_ready, quads + q + 1)
                    for ch in range(3):
                        n = 3 * q + ch
                        if n >= 2:
                            pe.wait_ge(hid_done, quads * 3 + n - 1)
                        for part in range(2):
                            mm = pe.matmul(pair[n % 2][:, part, :], w1[:, 3 * part + ch, :], xnT[:, :],
                                           start=True, stop=True)
                        mm.then_inc(up_done, 1)
                    pe.wait_ge(hid_done, quads * 3 + 3 * q + 3)
                    if q >= 1:
                        pe.wait_ge(layer_in, batches + B + QUAD * q)
                    for t in range(QUAD):
                        for ch in range(3):
                            mm = pe.matmul(psM[:, P * t:P * t + P], hid[:, ch, P * t:P * t + P], w2[:, ch, :],
                                           start=(ch == 0), stop=(ch == 2))
                    mm.then_inc(down_done, 1)


def store(c, src):
    with ExitStack() as ctx:
        stored = c.sem("stored")
        block = ctx.enter_context(c.nc.Block())

        @block.sync
        def _(sp):
            sp.dma_start(c.io["out"].rearrange("b t d -> t b d"), src).then_inc(stored, 16)
            sp.wait_ge(stored, 16)


STAGES = [first_attention, expert_ffn, second_attention, local_transformer]


def program(nc, io, upto=9):
    with ExitStack() as ctx:
        c = Core(nc, ctx, io)
        for stage in STAGES[:upto]:
            stage(c)
        store(c, c.X[:, :, :])


def constants():
    f = np.float32
    half = np.arange(0, DH, 2, dtype=f)
    t = np.arange(P, dtype=f)
    freqs = t[:, None] * (f(1.0) / f(10000.0) ** (half / f(DH)))[None, :]
    freqs = np.concatenate([freqs, freqs], -1).astype(f)
    base = (half + f(0.4 * DH)) / f(1.4 * DH)
    scale = base[None, :] ** ((t - P // 2) / f(WINDOW // 2))[:, None]
    scale = np.concatenate([scale, scale], -1).astype(f)
    sign = np.where(np.arange(DH) < DH // 2, f(-1.0), f(1.0))
    cos, sin = np.cos(freqs), np.sin(freqs) * sign
    rot = np.stack([cos * scale * f(QK_SCALE), cos / scale, sin * scale * f(QK_SCALE), sin / scale], 1)
    query = np.arange(P)[:, None]
    key = query // WINDOW * WINDOW - WINDOW + np.arange(2 * WINDOW)[None, :]
    masked = (query < key) | (query > key + WINDOW) | (key < 0)
    mask = np.where(masked, f(-3.0e38), f(0.0))
    return {
        "c_ident": np.eye(P, dtype=f),
        "c_shift": np.eye(P, k=1, dtype=f),
        "c_before": np.triu(np.ones((P, P), f), 1),
        "c_lower": np.tril(np.ones((EXPERTS, EXPERTS), f), -1),
        "c_mask": mask,
        "c_rot": rot.astype(f),
    }


def laid_out(inputs):
    w0 = np.zeros((P, 2, 4, 4, 32), np.float32)
    b0 = np.zeros((4, 32, 2, 2, 2), np.float32)
    for qk, name in enumerate("qk"):
        w0[:, qk, :, :, :DEPTH0] = np.asarray(inputs["L0_xattn_W" + name]).reshape(D, 4, 4, DEPTH0)
        b0[:, :DEPTH0, :, qk, :] = np.asarray(inputs["L0_xattn_b" + name]).reshape(2, 2, 4, DEPTH0).transpose(2, 3, 0, 1)
    def padded(a, axis):
        a = np.asarray(a)
        shape = list(a.shape)
        shape[axis] = 3 * P
        out = np.zeros(shape, a.dtype)
        out[tuple(slice(n) for n in a.shape)] = a
        return out

    w1 = np.asarray(inputs["L1_ffn_W1"]).reshape(LAYERS, D, 2, GLU)
    b1 = np.asarray(inputs["L1_ffn_b1"]).reshape(LAYERS, 2, GLU)
    cols = np.concatenate([padded(b1, 2).reshape(LAYERS, 6, P), np.asarray(inputs["L1_ffn_ln_g"])[:, None],
                           np.asarray(inputs["L1_ffn_ln_b"])[:, None]], 1)
    local = {
        "l_w1": padded(w1, 3).reshape(LAYERS, D, 6, P),
        "l_w2": padded(inputs["L1_ffn_W2"], 1).reshape(LAYERS, 3, P, D).transpose(0, 2, 1, 3),
        "l_cols": cols.transpose(0, 2, 1),
        "l_scales": np.stack([inputs["L1_ffn_q_scale"], inputs["L1_ffn_k_scale"]], 1),
    }
    local["l_wr"] = np.asarray(inputs["L0_ffn_Wr"]).T
    local["l_w1x"] = np.stack([np.asarray(inputs["L1_xattn_W" + n]).T for n in "qkvo"], 1)
    local["l_b1x"] = np.stack([inputs["L1_xattn_bq"], inputs["L1_xattn_bk"]], 1)
    return {**local, "l_w0_pad": w0.reshape(P, 2, 4, P), "l_b0_pad": b0.reshape(P, 2, 2, 2)}


def kernel(**inputs):
    import concourse.bacc as _bacc
    from concourse.bass_utils import run_bass_kernel_spmd as _run

    nc = _bacc.Bacc("TRN2", target_bir_lowering=False, num_devices=1)
    arrays, io = {}, {}
    for name, a in {**inputs, **laid_out(inputs), **constants()}.items():
        a = np.ascontiguousarray(a)
        arrays["in_" + name] = a
        io[name] = nc.dram_tensor("in_" + name, a.shape, mybir.dt.from_np(a.dtype), kind="ExternalInput").ap()
    io["out"] = nc.dram_tensor("out", (B, P, D), F32, kind="ExternalOutput").ap()
    program(nc, io)
    return _run(nc, [arrays], core_ids=[0]).results[0]["out"]
```

```python
from contextlib import ExitStack

import numpy as np

import concourse.bass as bass
from concourse import mybir

F32 = mybir.dt.float32
BF16 = mybir.dt.bfloat16
I32 = mybir.dt.int32
U32 = mybir.dt.uint32
ALU = mybir.AluOpType
ACT = mybir.ActivationFunctionType
AX = mybir.AxisListType

P = 128
B = 16
D = 128
HEADS = 16
UH = HEADS // 2
UNITS = 2 * B
BANK = 512
LN_EPS = 1e-5
FLT_MAX = float(np.finfo(np.float32).max)

DEPTH0 = D // HEADS
SCALE0 = float(DEPTH0) ** -0.5

EXPERTS = 8
FF = 512
TOPK = 2
ROWS = B * P * TOPK
CHUNK = ROWS // EXPERTS

SCALE1 = float(D) ** -0.5

LAYERS = 6
DH = 64
INNER = HEADS * DH
WINDOW = 32
GLU = 341
GCH = [(0, 128), (128, 128), (256, GLU - 256)]
QK_SCALE = 8.0
QUAD = 4
QUADS = B // QUAD


def units(eng, body, ahead, between={}):
    for i in range(4):
        body(i // 2, i, i, lambda k: i >= k)
    with eng.Fori(2, B - 3, 2) as b0:
        for s in range(4):
            body(b0 + s // 2, b0 * 2 + s, s, lambda k: True)
    for i in range(UNITS - 4, UNITS + ahead):
        body(i // 2, i, i % 4, lambda k: i - k < UNITS)
        if i in between:
            between[i]()


def one(b):
    return bass.ds(b, 1)


def row(ap):
    return ap.rearrange("p o d -> p (o d)")


class Core:

    def __init__(self, nc, ctx, io):
        self.nc, self.io = nc, io
        self.sems = ctx
        sb = lambda name, shape, dt=F32: ctx.enter_context(nc.sbuf_tensor(name, shape, dt))
        self.X = sb("X", [P, B, D])
        self.ident = sb("ident", [P, P])
        self.stats = sb("ln_stats", [P, B, 6])
        self.meanvar = sb("ln_meanvar", [P, B, 2])
        self.vareps = sb("ln_vareps", [P, B])
        self.rstd = sb("ln_rstd", [P, B])
        self.minus_half = sb("minus_half", [P, B])

    def sem(self, name):
        return self.sems.enter_context(self.nc.semaphore(name))


def ln_stats_dve(dve, c, stats_done, ln_step, X):
    for b in range(B):
        dve.bn_stats(c.stats[:, b, :], X[:, b, :]).then_inc(stats_done, 1)
    dve.wait_ge(stats_done, B)
    for b in range(B):
        dve.bn_aggr(c.meanvar[:, b, :], c.stats[:, b, :]).then_inc(stats_done, 1)
    dve.wait_ge(stats_done, 2 * B)
    dve.tensor_scalar(c.vareps[:, :], c.meanvar[:, :, 1], LN_EPS, None, ALU.add).then_inc(ln_step, 1)


def ln_rstd_pool(pool, c, ln_step, rstd_done):
    pool.memset(c.minus_half[:, :], -0.5).then_inc(rstd_done, 1)
    pool.wait_ge(rstd_done, 1)
    pool.wait_ge(ln_step, 1)
    pool.tensor_tensor(c.rstd[:, :], c.vareps[:, :], c.minus_half[:, :], ALU.pow).then_inc(rstd_done, 1)


def first_attention(c):
    nc, io = c.nc, c.io
    with ExitStack() as ctx:
        sb = lambda name, shape, dt=F32: ctx.enter_context(nc.sbuf_tensor("a_" + name, shape, dt))
        ps = lambda name, shape, dt=F32: ctx.enter_context(nc.psum_tensor("a_" + name, shape, dt))
        sem = lambda name: c.sem("a_" + name)
        X = c.X
        w_raw = sb("w_raw", [P, 2, D])
        w_pad = sb("w_pad", [P, 2, 4, P])
        b_pad = sb("b_pad", [P, 2, 2, 2])
        bv_all = sb("bv_all", [P, D])
        bo_all = sb("bo_all", [P, D])
        ctx_in = sb("ctx_in", [P, 2, D])
        xn_in = sb("xn_in", [P, 2, D])
        xcT = sb("xcT", [P, 2, 2, P])
        qkT = sb("qkT", [P, 2, 4, P])
        v1 = sb("v1", [P, 2, HEADS, 32])
        mx = sb("mx", [P, 2, UH])
        sd = sb("sd", [P, 2, UH, P])
        pr = sb("pr", [P, 2, UH, P])
        prT = sb("prT", [P, UH, P])
        rden = sb("rden", [P, UH])
        opT = sb("opT", [P, 2, P])
        on = sb("on", [P, 2, D])
        onT = sb("onT", [P, D])
        proj = sb("proj", [P, D])

        psT = ps("psT", [P, 4, P])
        psP = ps("psP", [P, 4, P])
        psPT = ps("psPT", [P, 4, P])
        psO = ps("psO", [P, 4, P])
        psS = ps("psS", [P, 4, 4, P])

        ld_w, ld_x, ld_ctx = sem("ld_w"), sem("ld_x"), [sem("ld_ctx0"), sem("ld_ctx1")]
        vones = sem("vones")
        stats_done, ln_step, rstd_done = sem("stats_done"), sem("ln_step"), sem("rstd_done")
        xn_ready, t_done, xcT_ready = sem("xn_ready"), sem("t_done"), sem("xcT_ready")
        qk_proj, qk_ready, v_proj, v_ready = sem("qk_proj"), sem("qk_ready"), sem("v_proj"), sem("v_ready")
        s_done, mx_done, sd_done, exp_done = sem("s_done"), sem("mx_done"), sem("sd_done"), sem("exp_done")
        pt_done, pt_ready, pv_done, rden_done = sem("pt_done"), sem("pt_ready"), sem("pv_done"), sem("rden_done")
        opT_ready, op_done = sem("opT_ready"), sem("op_done")
        on_done, onT_done, onT_ready = sem("on_done"), sem("onT_done"), sem("onT_ready")
        wo_done, proj_done, x_done = sem("wo_done"), sem("proj_done"), sem("x_done")

        block = ctx.enter_context(nc.Block())

        @block.sync
        def _(sp):
            sp.dma_start(X[:, :, :], io["x"].rearrange("b t d -> t b d")).then_inc(ld_x, 16)
            sp.dma_start(c.ident[:, :], io["c_ident"]).then_inc(ld_w, 16)
            sp.dma_start(w_pad[:, :, :, :], io["l_w0_pad"]).then_inc(ld_w, 16)
            sp.dma_start(b_pad[:, :, :, :], io["l_b0_pad"]).then_inc(ld_w, 16)
            for n, w in enumerate(("Wv", "Wo")):
                sp.dma_start(w_raw[:, n, :], io["L0_xattn_" + w]).then_inc(ld_w, 16)
            for b in range(2):
                sp.dma_start(ctx_in[:, b, :], io["ctx_1024"][b]).then_inc(ld_ctx[b], 16)
            sp.dma_start(bv_all[:, :], io["L0_xattn_bv"].partition_broadcast(P)).then_inc(ld_w, 16)
            sp.dma_start(bo_all[:, :], io["L0_xattn_bo"].partition_broadcast(P)).then_inc(ld_w, 16)
            with sp.Fori(0, B - 3, 2) as b0:
                for p in range(2):
                    sp.wait_ge(t_done, b0 + p + 1)
                    sp.dma_start(ctx_in[:, p, :], io["ctx_1024"][bass.ds(b0 + p + 2, 1), :, :]
                                 .rearrange("o t d -> t (o d)")).then_inc(ld_ctx[p], 16)

        @block.gpsimd
        def _(pool):
            pool.memset(v1[:, :, :, DEPTH0 + 1:], 0.0).then_inc(vones, 1)
            pool.memset(v1[:, :, :, DEPTH0:DEPTH0 + 1], 1.0).then_inc(vones, 1)
            ln_rstd_pool(pool, c, ln_step, rstd_done)

        @block.vector
        def _(dve):
            dve.wait_ge(ld_x, 16)
            ln_stats_dve(dve, c, stats_done, ln_step, X)
            dve.wait_ge(ld_w, 16 * 7)
            dve.wait_ge(rstd_done, 2)

            def stage(b, pb):
                dve.tensor_scalar(xn_in[:, pb, :], row(X[:, one(b), :]), c.meanvar[:, one(b), 0],
                                  c.rstd[:, one(b)], ALU.subtract, ALU.mult).then_inc(xn_ready, 1)

            stage(0, 0)
            dve.wait_ge(vones, 2)

            def body(b, i, s, live):
                u, pb = s % 2, s // 2
                if live(0):
                    dve.wait_ge(qk_proj, i + 1)
                    dve.tensor_tensor(qkT[:, u, :, :], psP[:, :, :],
                                      b_pad[:, u, :, :].rearrange("p a g -> p (a g)").unsqueeze(2)
                                      .to_broadcast([P, 4, P]), ALU.add).then_inc(qk_ready, 1)
                    if u == 0:
                        dve.wait_ge(v_proj, b + 1)
                        if live(3):
                            dve.wait_ge(op_done, i - 2)
                        dve.tensor_tensor(v1[:, pb, :, 0:DEPTH0],
                                          psO[:, 2, :].rearrange("p (n d) -> p n d", d=DEPTH0),
                                          bv_all[:, :].rearrange("p (n d) -> p n d", d=DEPTH0),
                                          ALU.add).then_inc(v_ready, 1)
                    elif live(-1):
                        if live(2):
                            dve.wait_ge(t_done, b)
                        stage(b + 1, 1 - pb)
                if live(3):
                    q = ((s - 3) % 4) // 2
                    o = psO[:, 0:2, :].rearrange("p g (n d) -> p (g n) d", d=32)
                    dve.wait_ge(op_done, i - 2)
                    dve.reciprocal(rden[:, :], o[:, :, DEPTH0]).then_inc(rden_done, 1)
                    dve.wait_ge(rden_done, i - 2)
                    dve.tensor_tensor(on[:, q, 64 * (1 - u):64 * (1 - u) + 64]
                                      .rearrange("p (n d) -> p n d", d=DEPTH0),
                                      o[:, :, 0:DEPTH0],
                                      rden[:, :].unsqueeze(2).to_broadcast([P, UH, DEPTH0]),
                                      ALU.mult).then_inc(on_done, 1)
                if live(1):
                    v = 1 - u
                    dve.wait_ge(s_done, i)
                    dve.tensor_reduce(mx[:, v, :].rearrange("p (h g) -> p h g", h=4), psS[:, :, 0:2, :],
                                      AX.X, ALU.max).then_inc(mx_done, 1)
                    dve.wait_ge(mx_done, i)
                    dve.tensor_tensor(sd[:, v, :, :].rearrange("p (h g) k -> p h g k", h=4), psS[:, :, 0:2, :],
                                      mx[:, v, :].rearrange("p (h g) -> p h g", h=4).unsqueeze(3)
                                      .to_broadcast([P, 4, 2, P]), ALU.subtract).then_inc(sd_done, 1)
                if live(4) and u == 0:
                    dve.wait_ge(wo_done, b - 1)
                    dve.tensor_tensor(proj[:, :], psT[:, 3, :], bo_all[:, :], ALU.add).then_inc(proj_done, 1)
                    dve.wait_ge(proj_done, b - 1)
                    dve.tensor_tensor(row(X[:, one(b - 2), :]), proj[:, :], row(X[:, one(b - 2), :]),
                                      ALU.add).then_inc(x_done, 1)

            units(dve, body, 3)
            dve.wait_ge(x_done, B)

        @block.scalar
        def _(act):
            def evac_xc(b, pb):
                act.wait_ge(t_done, b + 1)
                act.activation(xcT[:, pb, :, :], psT[:, 0:2, :], ACT.Copy)\
                   .then_inc(xcT_ready, 1)

            evac_xc(0, 0)

            def body(b, i, s, live):
                u, pb = s % 2, s // 2
                if live(4) and u == 0:
                    act.wait_ge(onT_done, b - 1)
                    act.activation(onT[:, :], psT[:, 2, :], ACT.Copy).then_inc(onT_ready, 1)
                if live(2):
                    for part, bank in enumerate((psPT, psP)):
                        act.wait_ge(pt_done, i * 2 - 3 + part)
                        act.activation(prT[:, 4 * part:4 * part + 4, :], bank[:, :, :], ACT.Copy)\
                           .then_inc(pt_ready, 1)
                if live(0) and u == 1 and live(-1):
                    evac_xc(b + 1, 1 - pb)
                if live(2):
                    act.wait_ge(pv_done, i - 1)
                    act.activation(opT[:, :, :], psO[:, 0:2, :], ACT.Copy).then_inc(opT_ready, 1)
                if live(1):
                    act.wait_ge(sd_done, i)
                    act.activation(pr[:, 1 - u, :, :], sd[:, 1 - u, :, :], ACT.Exp, scale=SCALE0)\
                       .then_inc(exp_done, 1)

            units(act, body, 3)

        @block.tensor
        def _(pe):
            pe.wait_ge(ld_w, 16 * 7)

            def transposes(b, pb):
                pe.wait_ge(xn_ready, b + 1)
                pe.wait_ge(ld_ctx[pb], b * 8 + 16 - 8 * pb)
                pe.transpose(psT[:, 0, :], xn_in[:, pb, :], c.ident[:, :])
                pe.transpose(psT[:, 1, :], ctx_in[:, pb, :], c.ident[:, :]).then_inc(t_done, 1)

            transposes(0, 0)

            def body(b, i, s, live):
                u, pb = s % 2, s // 2
                if live(0):
                    pe.wait_ge(xcT_ready, b + 1)
                    if live(1):
                        pe.wait_ge(qk_ready, i)
                    if live(3):
                        pe.wait_ge(pt_ready, i * 2 - 4)
                    for qk in range(2):
                        for g in range(2):
                            mm = pe.matmul(psP[:, 2 * qk + g, :], w_pad[:, qk, 2 * u + g, :],
                                           xcT[:, pb, qk, :], start=True, stop=True)
                    mm.then_inc(qk_proj, 1)
                    if u == 0:
                        if live(3):
                            pe.wait_ge(opT_ready, i - 2)
                        pe.matmul(psO[:, 2, :], xcT[:, pb, 1, :], w_raw[:, 0, :],
                                  start=True, stop=True).then_inc(v_proj, 1)
                if live(3):
                    pe.wait_ge(opT_ready, i - 2)
                    for g in range(2):
                        mm = pe.transpose(psO[:, g, :], opT[:, g, :], c.ident[:, :])
                    mm.then_inc(op_done, 1)
                if live(1):
                    v = 1 - u
                    pe.wait_ge(qk_ready, i)
                    if live(2):
                        pe.wait_ge(sd_done, i - 1)
                    for g in range(2):
                        for blk in range(4):
                            r = slice(32 * blk, 32 * blk + 32)
                            mm = pe.matmul(psS[:, blk, g, :], qkT[r, v, g, :], qkT[r, v, 2 + g, :],
                                           start=True, stop=True)
                    mm.then_inc(s_done, 1)
                if live(4) and u == 0:
                    pe.wait_ge(on_done, i - 2)
                    if not live(0):
                        pe.wait_ge(proj_done, b - 2)
                    pe.transpose(psT[:, 2, :], on[:, pb, :], c.ident[:, :]).then_inc(onT_done, 1)
                if live(2):
                    pe.wait_ge(exp_done, i - 1)
                    for part, bank in enumerate((psPT, psP)):
                        if part == 1 and live(0):
                            pe.wait_ge(qk_ready, i + 1)
                        for n in range(4):
                            mm = pe.transpose(bank[:, n, :], pr[:, u, 4 * part + n, :], c.ident[:, :])
                        mm.then_inc(pt_done, 1)
                if live(4) and u == 0:
                    pe.wait_ge(onT_ready, b - 1)
                    pe.matmul(psT[:, 3, :], onT[:, :], w_raw[:, 1, :], start=True, stop=True).then_inc(wo_done, 1)
                if live(0) and u == 1 and live(-1):
                    if live(4):
                        pe.wait_ge(proj_done, b - 1)
                    transposes(b + 1, 1 - pb)
                if live(2):
                    q = ((s - 2) % 4) // 2
                    if live(0) and u == 0:
                        pe.wait_ge(v_ready, b + 1)
                    if live(3):
                        pe.wait_ge(on_done, i - 2)
                    for part in range(2):
                        pe.wait_ge(pt_ready, i * 2 - 3 + part)
                        for g in range(2):
                            for blk in (2 * part, 2 * part + 1):
                                mm = pe.matmul(psO[32 * blk:32 * blk + 32, g, :], v1[:, q, UH * u + 4 * g + blk, :],
                                               prT[:, 2 * blk + g, :], start=True, stop=True)
                    mm.then_inc(pv_done, 1)

            units(pe, body, 3)


def expert_ffn(c):
    nc, io = c.nc, c.io
    with ExitStack() as ctx:
        sb = lambda name, shape, dt=F32: ctx.enter_context(nc.sbuf_tensor("b_" + name, shape, dt))
        ps = lambda name, shape, dt=F32: ctx.enter_context(nc.psum_tensor("b_" + name, shape, dt))
        sem = lambda name: c.sem("b_" + name)
        X, E, T4 = c.X, EXPERTS, CHUNK // P
        sorted_rows = nc.dram_tensor("b_sorted_rows", [ROWS, D], F32, kind="Internal").ap()
        expert_out = nc.dram_tensor("b_expert_out", [ROWS, D], F32, kind="Internal").ap()

        xn = sb("xn", [P, B, D])
        xnT = sb("xnT", [P, 2, QUAD, P])
        wrT = sb("wrT", [P, E])
        before = sb("before", [P, P])
        ones = sb("ones", [P, P])
        lower = sb("lower", [P, E, E])
        lg = sb("lg", [P, B, E])
        gt = sb("gt", [P, B, E, E])
        eq = sb("eq", [P, B, E, E])
        eql = sb("eql", [P, B, E, E])
        cnt = sb("cnt", [P, B, E, E])
        rank = sb("rank", [P, B, E])
        chosen = sb("chosen", [P, B, E])
        sel = sb("sel", [P, 2, B, E])
        tot = sb("tot", [P, E, B])
        scan = sb("scan", [P, E * B])
        start = sb("start", [P, E, B])
        pos = sb("pos", [P, B, E])
        pick = sb("pick", [P, 2, 2, B, E])
        picked = sb("picked", [P, 2, 2, B])
        where = sb("where", [P, 2, B], U32)
        dl = sb("dl", [P, B])
        ex = sb("ex", [P, B])
        den = sb("den", [P, B])
        wt = sb("wt", [P, 2, B])

        rows = sb("rows", [P, 2, T4, P])
        w1 = sb("w1", [P, 2, FF])
        w2 = sb("w2", [P, 2, FF // P, D])
        rowsT = sb("rowsT", [P, CHUNK])
        hid = sb("hid", [P, 2, FF // P, CHUNK])
        eo = sb("eo", [P, 2, T4 * D])
        got = sb("got", [P, 2, B, D])

        psT = ps("psT", [P, 4, P])
        psL = ps("psL", [P, BANK])
        psC = ps("psC", [P, BANK])
        psH = ps("psH", [P, FF // P, BANK])
        psY = ps("psY", [P, BANK])

        ld_c, ld_w, ld_r = sem("ld_c"), [sem("ld_w0"), sem("ld_w1")], [sem("ld_r0"), sem("ld_r1")]
        stats_done, ln_step, rstd_done = sem("stats_done"), sem("ln_step"), sem("rstd_done")
        xn_done, t_done, xnT_ready, lg_done = sem("xn_done"), sem("t_done"), sem("xnT_ready"), sem("lg_done")
        route = sem("route")
        choice_ready, count_done, dl_ready, ex_done = sem("choice_ready"), sem("count_done"), sem("dl_ready"), sem("ex_done")
        where_ready, scattered = sem("where_ready"), sem("scattered")
        rT_done, rT_ready, up_done, hid_ready = sem("rT_done"), sem("rT_ready"), sem("up_done"), sem("hid_ready")
        down_done, eo_ready, eo_out = sem("down_done"), sem("eo_ready"), [sem("eo_out0"), sem("eo_out1")]
        gathered, x_step = [sem("gathered%d" % q) for q in range(QUADS)], sem("x_step")

        block = ctx.enter_context(nc.Block())

        @block.sync
        def _(sp):
            sp.dma_start(wrT[:, :], io["l_wr"]).then_inc(ld_c, 16)
            sp.dma_start(before[:, :], io["c_before"]).then_inc(ld_c, 16)
            sp.dma_start(lower[:, :, :], io["c_lower"].partition_broadcast(P)).then_inc(ld_c, 16)

            def load_weights(e, p):
                sp.dma_start(w1[:, p, :], io["L0_ffn_W1"][one(e), :, :].rearrange("o k n -> k (o n)"))\
                  .then_inc(ld_w[p], 16)
                sp.dma_start(w2[:, p, :, :], io["L0_ffn_W2"][one(e), :, :].rearrange("o (c k) n -> k (o c) n", k=P))\
                  .then_inc(ld_w[p], 16)

            def load_rows(e, p):
                src = sorted_rows.rearrange("(e t p) d -> e p t d", e=E, p=P)
                sp.dma_start(rows[:, p, :, :], src[one(e), :, :, :].rearrange("o p t d -> p (o t) d"))\
                  .then_inc(ld_r[p], 16)

            def store_out(e, p):
                dst = expert_out.rearrange("(e t p) d -> e p t d", e=E, p=P)
                sp.dma_start(dst[one(e), :, :, :].rearrange("o p t d -> p (o t) d"),
                             eo[:, p, :].rearrange("p (t d) -> p t d", d=D)).then_inc(eo_out[p], 16)

            for e in range(2):
                load_weights(e, e)
            sp.wait_ge(scattered, 16 * TOPK * B)
            for e in range(2):
                load_rows(e, e)
            with sp.Fori(0, E - 3, 2) as e0:
                for p in range(2):
                    sp.wait_ge(rT_done, e0 + p + 1)
                    load_rows(e0 + p + 2, p)
                    sp.wait_ge(down_done, e0 + p + 1)
                    load_weights(e0 + p + 2, p)
                    sp.wait_ge(eo_ready, e0 + p + 1)
                    store_out(e0 + p, p)
            for e in range(E - 2, E):
                sp.wait_ge(eo_ready, e + 1)
                store_out(e, e % 2)
            for p in range(2):
                sp.wait_ge(eo_out[p], 16 * E // 2)

        @block.gpsimd
        def _(pool):
            pool.memset(ones[:, :], 1.0).then_inc(ld_c, 16)
            ln_rstd_pool(pool, c, ln_step, rstd_done)
            pool.wait_ge(xn_done, B)
            for b in range(B):
                for k in range(TOPK):
                    pool.wait_ge(where_ready, 2)
                    pool.indirect_dma_start(
                        out=sorted_rows, out_offset=bass.IndirectOffsetOnAxis(ap=where[:, k, b:b + 1], axis=0),
                        in_=xn[:, b, :], in_offset=None).then_inc(scattered, 16)
            for p in range(2):
                pool.wait_ge(eo_out[p], 16 * E // 2)
            for b in range(B):
                for k in range(TOPK):
                    pool.indirect_dma_start(
                        out=got[:, k, b, :], out_offset=None, in_=expert_out,
                        in_offset=bass.IndirectOffsetOnAxis(ap=where[:, k, b:b + 1], axis=0))\
                        .then_inc(gathered[b // QUAD], 16)

        @block.vector
        def _(dve):
            ln_stats_dve(dve, c, stats_done, ln_step, X)
            dve.wait_ge(rstd_done, 2)
            for b in range(B):
                dve.tensor_scalar(xn[:, b, :], X[:, b, :], c.meanvar[:, b, 0:1], c.rstd[:, b:b + 1],
                                  ALU.subtract, ALU.mult).then_inc(xn_done, 1)

            steps = [0]

            def then(ins):
                steps[0] += 1
                ins.then_inc(route, 1)
                dve.wait_ge(route, steps[0])

            dve.wait_ge(lg_done, B)
            dve.wait_ge(ld_c, 64)
            then(dve.tensor_copy(lg[:, :, :].rearrange("p b e -> p (b e)"), psL[:, 0:B * E]))
            flat = lambda a: a.rearrange("p b e f -> p b (e f)")
            mine = lg[:, :, :].unsqueeze(3).to_broadcast([P, B, E, E])
            other = lg[:, :, :].unsqueeze(2).to_broadcast([P, B, E, E])
            dve.tensor_tensor(gt[:, :, :, :], other, mine, ALU.is_gt).then_inc(route, 1)
            then(dve.tensor_tensor(eq[:, :, :, :], other, mine, ALU.is_equal))
            steps[0] += 1
            dve.wait_ge(route, steps[0])
            then(dve.tensor_tensor(flat(eql[:, :, :, :]), flat(eq[:, :, :, :]),
                                   lower[:, :, :].rearrange("p e f -> p (e f)").unsqueeze(1)
                                   .to_broadcast([P, B, E * E]), ALU.mult))
            then(dve.tensor_tensor(cnt[:, :, :, :], gt[:, :, :, :], eql[:, :, :, :], ALU.add))
            then(dve.tensor_reduce(rank[:, :, :], cnt[:, :, :, :], AX.X, ALU.add))
            dve.tensor_scalar(chosen[:, :, :], rank[:, :, :], TOPK - 0.5, None, ALU.is_lt).then_inc(choice_ready, 1)
            for k in range(TOPK):
                dve.tensor_scalar(sel[:, k, :, :], rank[:, :, :], float(k), None, ALU.is_equal)\
                   .then_inc(choice_ready, 1)
            dve.wait_ge(choice_ready, 3)
            for k in range(TOPK):
                dve.tensor_tensor(pick[:, 1, k, :, :], sel[:, k, :, :], lg[:, :, :], ALU.mult)\
                   .then_inc(choice_ready, 1)
            dve.wait_ge(count_done, 1)
            then(dve.tensor_copy(tot[:, :, :], psC[:, P:2 * P].rearrange("p (b e) -> p e b", e=E)))
            flat_tot = tot[:, :, :].rearrange("p e b -> p (e b)")
            then(dve.tensor_tensor_scan(scan[:, :], ones[:, :], flat_tot, 0.0, ALU.mult, ALU.add))
            then(dve.tensor_tensor(start[:, :, :].rearrange("p e b -> p (e b)"), scan[:, :], flat_tot, ALU.subtract))
            then(dve.tensor_tensor(pos[:, :, :], psC[:, 0:P].rearrange("p (b e) -> p b e", e=E),
                                   start[:, :, :].rearrange("p e b -> p b e"), ALU.add))
            for k in range(TOPK):
                dve.tensor_tensor(pick[:, 0, k, :, :], sel[:, k, :, :], pos[:, :, :], ALU.mult)\
                   .then_inc(choice_ready, 1)
            dve.wait_ge(choice_ready, 7)
            then(dve.tensor_reduce(picked[:, :, :, :].rearrange("p a k b -> p (a k) b"),
                                   pick[:, :, :, :, :].rearrange("p a k b e -> p (a k) b e"), AX.X, ALU.add))
            for k in range(TOPK):
                dve.tensor_copy(where[:, k, :], picked[:, 0, k, :]).then_inc(where_ready, 1)
            dve.tensor_tensor(dl[:, :], picked[:, 1, 1, :], picked[:, 1, 0, :], ALU.subtract).then_inc(dl_ready, 1)
            dve.wait_ge(ex_done, 1)
            then(dve.tensor_scalar(den[:, :], ex[:, :], 1.0, None, ALU.add))
            then(dve.reciprocal(wt[:, 0, :], den[:, :]))
            then(dve.tensor_tensor(wt[:, 1, :], wt[:, 0, :], ex[:, :], ALU.mult))

            def rows_transposed(e):
                dve.wait_ge(rT_done, e + 1)
                dve.tensor_scalar(rowsT[:, :], psT[:, :, :].rearrange("p t n -> p (t n)"), 1.0, None, ALU.mult)\
                   .then_inc(rT_ready, 1)

            def result(e, p, stores):
                dve.wait_ge(down_done, e + 1)
                if stores is not None:
                    dve.wait_ge(eo_out[p], stores)
                dve.tensor_scalar(eo[:, p, :], psY[:, :], 1.0, None, ALU.mult).then_inc(eo_ready, 1)

            rows_transposed(0)
            with dve.Fori(0, E - 3, 2) as e0:
                for p in range(2):
                    rows_transposed(e0 + p + 1)
                    result(e0 + p, p, e0 * 8 if p else None)
            rows_transposed(E - 1)
            result(E - 2, 0, 8 * (E - 2))
            result(E - 1, 1, 8 * (E - 2))

            for q in range(QUADS):
                dve.wait_ge(gathered[q], 16 * TOPK * QUAD)
                for k in range(TOPK):
                    if k:
                        dve.wait_ge(x_step, QUAD * (TOPK * q + 1))
                    for b in range(QUAD * q, QUAD * q + QUAD):
                        dve.scalar_tensor_tensor(out=X[:, b, :], in0=got[:, k, b, :], scalar=wt[:, k, b:b + 1],
                                                 in1=X[:, b, :], op0=ALU.mult, op1=ALU.add).then_inc(x_step, 1)
            dve.wait_ge(x_step, 2 * B)

        @block.scalar
        def _(act):
            for q in range(QUADS):
                act.wait_ge(t_done, q + 1)
                act.activation(xnT[:, q % 2, :, :], psT[:, :, :], ACT.Copy).then_inc(xnT_ready, 1)
            act.wait_ge(dl_ready, 1)
            act.activation(ex[:, :], dl[:, :], ACT.Exp).then_inc(ex_done, 1)
            with act.Fori(0, E - 1, 2) as e0:
                for p in range(2):
                    for f in range(FF // P):
                        act.wait_ge(up_done, e0 * 4 + 4 * p + f + 1)
                        act.activation(hid[:, p, f, :], psH[:, f, :], ACT.Gelu).then_inc(hid_ready, 1)

        @block.tensor
        def _(pe):
            pe.wait_ge(ld_c, 64)
            for q in range(QUADS):
                pe.wait_ge(xn_done, QUAD * q + QUAD)
                if q:
                    pe.wait_ge(xnT_ready, q)
                for t in range(QUAD):
                    mm = pe.transpose(psT[:, t, :], xn[:, QUAD * q + t, :], c.ident[:, :])
                mm.then_inc(t_done, 1)
                pe.wait_ge(xnT_ready, q + 1)
                for t in range(QUAD):
                    b = QUAD * q + t
                    pe.matmul(psL[:, E * b:E * b + E], xnT[:, q % 2, t, :], wrT[:, :], start=True, stop=True)\
                      .then_inc(lg_done, 1)
            pe.wait_ge(choice_ready, 3)
            ch = chosen[:, :, :].rearrange("p b e -> p (b e)")
            pe.matmul(psC[:, 0:P], before[:, :], ch, start=True, stop=True)
            pe.matmul(psC[:, P:2 * P], ones[:, :], ch, start=True, stop=True).then_inc(count_done, 1)

            def rows_in(e, p):
                pe.wait_ge(ld_r[p], e * 8 + 16 - 8 * p)
                for t in range(T4):
                    mm = pe.transpose(psT[:, t, :], rows[:, p, t, :], c.ident[:, :])
                mm.then_inc(rT_done, 1)

            def up(e, p):
                pe.wait_ge(ld_w[p], e * 16 + 32 - 16 * p)
                pe.wait_ge(rT_ready, e + 1)
                for f in range(FF // P):
                    pe.matmul(psH[:, f, :], w1[:, p, P * f:P * f + P], rowsT[:, :], start=True, stop=True)\
                      .then_inc(up_done, 1)

            def down(e, p, first):
                pe.wait_ge(hid_ready, e * 4 + 4)
                if not first:
                    pe.wait_ge(eo_ready, e)
                for t in range(T4):
                    for f in range(FF // P):
                        mm = pe.matmul(psY[:, D * t:D * t + D], hid[:, p, f, P * t:P * t + P], w2[:, p, f, :],
                                       start=(f == 0), stop=(f == FF // P - 1))
                mm.then_inc(down_done, 1)

            rows_in(0, 0)
            up(0, 0)
            rows_in(1, 1)
            down(0, 0, True)
            up(1, 1)
            with pe.Fori(2, E - 1, 2) as e0:
                for p in range(2):
                    rows_in(e0 + p, p)
                    down(e0 + p - 1, 1 - p, False)
                    up(e0 + p, p)
            down(E - 1, 1, False)


def second_attention(c):
    nc, io = c.nc, c.io
    with ExitStack() as ctx:
        sb = lambda name, shape, dt=F32: ctx.enter_context(nc.sbuf_tensor("c_" + name, shape, dt))
        ps = lambda name, shape, dt=F32: ctx.enter_context(nc.psum_tensor("c_" + name, shape, dt))
        sem = lambda name: c.sem("c_" + name)
        X = c.X
        ctx_in = sb("ctx_in", [P, B, D])
        xn = sb("xn", [P, B, D])
        w = sb("w", [P, 4, D])
        bqk = sb("bqk", [P, 2])
        bv = sb("bv", [P, D])
        bo = sb("bo", [P, D])
        xnT = sb("xnT", [P, QUAD, P])
        ctxT = sb("ctxT", [P, QUAD, P])
        qT = sb("qT", [P, QUAD, P])
        kT = sb("kT", [P, QUAD, P])
        v = sb("v", [P, 2, QUAD, D])
        mx = sb("mx", [P, QUAD])
        sd = sb("sd", [P, QUAD, P])
        pr = sb("pr", [P, 2, QUAD, P])
        den = sb("den", [P, QUAD])
        rden = sb("rden", [P, 2, QUAD])
        prT = sb("prT", [P, QUAD, P])
        att = sb("att", [P, QUAD, D])
        res = sb("res", [P, QUAD, D])
        resT = sb("resT", [P, QUAD, P])
        proj = sb("proj", [P, QUAD, D])

        psX, psC, psQ, psK, psV, psS, psB0, psB1 = (ps(n, [P, 4, P]) for n in
                                                    ("psX", "psC", "psQ", "psK", "psV", "psS", "psB0", "psB1"))
        ld = sem("ld")
        stats_done, ln_step, rstd_done, xn_done = sem("stats_done"), sem("ln_step"), sem("rstd_done"), sem("xn_done")
        tx_done, tc_done, xnT_ready, ctxT_ready = sem("tx_done"), sem("tc_done"), sem("xnT_ready"), sem("ctxT_ready")
        q_done, k_done, v_done = sem("q_done"), sem("k_done"), sem("v_done")
        q_ready, k_ready, v_ready = sem("q_ready"), sem("k_ready"), sem("v_ready")
        s_done, mx_done, sd_done, exp_done = sem("s_done"), sem("mx_done"), sem("sd_done"), sem("exp_done")
        den_done, rden_done, pT_done, pT_ready = sem("den_done"), sem("rden_done"), sem("pT_done"), sem("pT_ready")
        a_done, att_done, res_done = sem("a_done"), sem("att_done"), sem("res_done")
        rT_done, rT_ready, o_done, proj_done, x_done = (sem("rT_done"), sem("rT_ready"), sem("o_done"),
                                                        sem("proj_done"), sem("x_done"))
        block = ctx.enter_context(nc.Block())

        @block.sync
        def _(sp):
            sp.dma_start(ctx_in[:, :, :], io["ctx_1024"].rearrange("b t d -> t b d")).then_inc(ld, 16)
            sp.dma_start(w[:, :, :], io["l_w1x"]).then_inc(ld, 16)
            sp.dma_start(bqk[:, :], io["l_b1x"]).then_inc(ld, 16)
            sp.dma_start(bv[:, :], io["L1_xattn_bv"].partition_broadcast(P)).then_inc(ld, 16)
            sp.dma_start(bo[:, :], io["L1_xattn_bo"].partition_broadcast(P)).then_inc(ld, 16)

        @block.gpsimd
        def _(pool):
            ln_rstd_pool(pool, c, ln_step, rstd_done)

        @block.vector
        def _(dve):
            ln_stats_dve(dve, c, stats_done, ln_step, X)
            dve.wait_ge(rstd_done, 2)
            for b in range(B):
                dve.tensor_scalar(xn[:, b, :], X[:, b, :], c.meanvar[:, b, 0:1], c.rstd[:, b:b + 1],
                                  ALU.subtract, ALU.mult).then_inc(xn_done, 1)
            dve.wait_ge(ld, 80)

            def front(q):
                dve.wait_ge(tc_done, q + 1)
                dve.tensor_copy(ctxT[:, :, :], psC[:, :, :]).then_inc(ctxT_ready, 1)
                dve.wait_ge(q_done, q + 1)
                dve.tensor_scalar(qT[:, :, :], psQ[:, :, :], bqk[:, 0:1], None, ALU.add).then_inc(q_ready, 1)
                dve.wait_ge(v_done, q + 1)
                dve.tensor_tensor(v[:, q % 2, :, :], psV[:, :, :], bv[:, :].unsqueeze(1).to_broadcast([P, QUAD, D]),
                                  ALU.add).then_inc(v_ready, 1)
                dve.wait_ge(s_done, q + 1)
                dve.tensor_reduce(mx[:, :], psS[:, :, :], AX.X, ALU.max).then_inc(mx_done, 1)
                dve.wait_ge(mx_done, q + 1)
                dve.tensor_tensor(sd[:, :, :], psS[:, :, :], mx[:, :].unsqueeze(2).to_broadcast([P, QUAD, P]),
                                  ALU.subtract).then_inc(sd_done, 1)
                dve.wait_ge(exp_done, q + 1)
                dve.tensor_reduce(den[:, :], pr[:, q % 2, :, :], AX.X, ALU.add).then_inc(den_done, 1)
                dve.wait_ge(den_done, q + 1)
                dve.reciprocal(rden[:, q % 2, :], den[:, :]).then_inc(rden_done, 1)

            def back(q):
                dve.wait_ge(a_done, q + 1)
                dve.wait_ge(rden_done, q + 1)
                dve.tensor_tensor(att[:, :, :], psB1[:, :, :], rden[:, q % 2, :].unsqueeze(2)
                                  .to_broadcast([P, QUAD, D]), ALU.mult).then_inc(att_done, 1)
                dve.wait_ge(att_done, q + 1)
                dve.tensor_tensor(res[:, :, :], att[:, :, :], xn[:, QUAD * q:QUAD * q + QUAD, :], ALU.add)\
                   .then_inc(res_done, 1)
                dve.wait_ge(o_done, q + 1)
                dve.tensor_tensor(proj[:, :, :], psB1[:, :, :], bo[:, :].unsqueeze(1).to_broadcast([P, QUAD, D]),
                                  ALU.add).then_inc(proj_done, 1)
                dve.wait_ge(proj_done, q + 1)
                xq = X[:, QUAD * q:QUAD * q + QUAD, :]
                dve.tensor_tensor(xq, proj[:, :, :], xq, ALU.add).then_inc(x_done, 1)

            front(0)
            for q in range(QUADS):
                if q + 1 < QUADS:
                    front(q + 1)
                back(q)
            dve.wait_ge(x_done, QUADS)

        @block.scalar
        def _(act):
            act.wait_ge(ld, 80)

            def front(q):
                act.wait_ge(tx_done, q + 1)
                act.activation(xnT[:, :, :], psX[:, :, :], ACT.Copy).then_inc(xnT_ready, 1)
                act.wait_ge(k_done, q + 1)
                act.activation(kT[:, :, :], psK[:, :, :], ACT.Identity, bias=bqk[:, 1:2]).then_inc(k_ready, 1)
                act.wait_ge(sd_done, q + 1)
                act.activation(pr[:, q % 2, :, :], sd[:, :, :], ACT.Exp, scale=SCALE1).then_inc(exp_done, 1)

            def back(q):
                act.wait_ge(pT_done, q + 1)
                act.activation(prT[:, :, :], psB0[:, :, :], ACT.Copy).then_inc(pT_ready, 1)
                act.wait_ge(rT_done, q + 1)
                act.activation(resT[:, :, :], psB0[:, :, :], ACT.Copy).then_inc(rT_ready, 1)

            front(0)
            for q in range(QUADS):
                if q + 1 < QUADS:
                    front(q + 1)
                back(q)

        @block.tensor
        def _(pe):
            pe.wait_ge(ld, 80)

            def front(q):
                pe.wait_ge(xn_done, QUAD * q + QUAD)
                if q:
                    pe.wait_ge(sd_done, q)
                for t in range(QUAD):
                    mm = pe.transpose(psX[:, t, :], xn[:, QUAD * q + t, :], c.ident[:, :])
                mm.then_inc(tx_done, 1)
                for t in range(QUAD):
                    mm = pe.transpose(psC[:, t, :], ctx_in[:, QUAD * q + t, :], c.ident[:, :])
                mm.then_inc(tc_done, 1)
                pe.wait_ge(xnT_ready, q + 1)
                pe.matmul(psQ[:, :, :].rearrange("p t n -> p (t n)"), w[:, 0, :],
                          xnT[:, :, :].rearrange("p t n -> p (t n)"), start=True, stop=True).then_inc(q_done, 1)
                pe.wait_ge(ctxT_ready, q + 1)
                pe.matmul(psK[:, :, :].rearrange("p t n -> p (t n)"), w[:, 1, :],
                          ctxT[:, :, :].rearrange("p t n -> p (t n)"), start=True, stop=True).then_inc(k_done, 1)
                for t in range(QUAD):
                    mm = pe.matmul(psV[:, t, :], ctxT[:, t, :], w[:, 2, :], start=True, stop=True)
                mm.then_inc(v_done, 1)
                pe.wait_ge(q_ready, q + 1)
                pe.wait_ge(k_ready, q + 1)
                for t in range(QUAD):
                    mm = pe.matmul(psS[:, t, :], qT[:, t, :], kT[:, t, :], start=True, stop=True)
                mm.then_inc(s_done, 1)

            def back(q):
                pe.wait_ge(exp_done, q + 1)
                if q:
                    pe.wait_ge(rT_ready, q)
                for t in range(QUAD):
                    mm = pe.transpose(psB0[:, t, :], pr[:, q % 2, t, :], c.ident[:, :])
                mm.then_inc(pT_done, 1)
                pe.wait_ge(pT_ready, q + 1)
                pe.wait_ge(v_ready, q + 1)
                if q:
                    pe.wait_ge(proj_done, q)
                for t in range(QUAD):
                    mm = pe.matmul(psB1[:, t, :], prT[:, t, :], v[:, q % 2, t, :], start=True, stop=True)
                mm.then_inc(a_done, 1)
                pe.wait_ge(res_done, q + 1)
                for t in range(QUAD):
                    mm = pe.transpose(psB0[:, t, :], res[:, t, :], c.ident[:, :])
                mm.then_inc(rT_done, 1)
                pe.wait_ge(rT_ready, q + 1)
                for t in range(QUAD):
                    mm = pe.matmul(psB1[:, t, :], resT[:, t, :], w[:, 3, :], start=True, stop=True)
                mm.then_inc(o_done, 1)

            front(0)
            for q in range(QUADS):
                if q + 1 < QUADS:
                    front(q + 1)
                back(q)


def local_transformer(c):
    nc, io = c.nc, c.io
    with ExitStack() as ctx:
        sb = lambda name, shape, dt=F32: ctx.enter_context(nc.sbuf_tensor("d_" + name, shape, dt))
        ps = lambda name, shape, dt=F32: ctx.enter_context(nc.psum_tensor("d_" + name, shape, dt))
        sem = lambda name: c.sem("d_" + name)
        X = c.X
        KEYS = 2 * WINDOW
        WINDOWS = P // WINDOW
        HALF = D // 2

        Y = sb("Y", [P, B, D])
        w_qkv = sb("w_qkv", [P, 3 * INNER])
        w_o = sb("w_o", [P, INNER // P, D])
        w1 = sb("w1", [P, 6, P])
        w2 = sb("w2", [P, 3, D])
        cols = sb("cols", [P, 8])
        b2 = sb("b2", [P, D])
        scales = sb("scales", [P, LAYERS, 2, DH])
        rot = sb("rot", [P, 4, DH])
        tab = sb("tab", [P, 4, DH])
        mask_in = sb("mask_in", [P, KEYS])
        mask = sb("mask", [P, 4 * KEYS], BF16)
        ident_bf = sb("ident_bf", [P, P], BF16)
        shift = sb("shift", [P, P])

        y_in = sb("y_in", [P, D])
        xsT = sb("xsT", [P, P])
        sq = sb("sq", [P, 2 * UH, DH])
        ss = sb("ss", [P, 2, 2 * UH])
        rn = sb("rn", [P, 2, 2 * UH])
        mhalf = sb("mhalf", [P, 2 * UH])
        raw = sb("raw", [P, 2, 2 * UH, DH])
        tc = sb("tc", [P, 2, 2 * UH, DH])
        ts = sb("ts", [P, 2, 2 * UH, DH])
        rs = sb("rs", [P, 2 * UH, DH])
        qr = sb("qr", [P, 2, 2 * UH * DH])
        qT = sb("qT", [P, 4, P])
        kT = sb("kT", [P, 4, WINDOW + P])
        v1 = sb("v1", [P, 4, UH, DH])
        mx = sb("mx", [P, 2, 4])
        sd = sb("sd", [P, 2, 2, 4, KEYS])
        pr = sb("pr", [P, 2, 2, 4, P])
        prT = sb("prT", [P, 2, 4, P])
        den = sb("den", [P, UH])
        rden = sb("rden", [P, UH])
        oT = sb("oT", [P, INNER // P, P])

        xs = sb("xs", [P, 2, QUAD, D])
        xn = sb("xn", [P, 2, QUAD, D])
        xnT = sb("xnT", [P, 2, QUAD * P])
        gate = sb("gate", [P, 2, QUAD * P])
        hid = sb("hid", [P, 2, 3, QUAD * P])
        yb = sb("yb", [P, QUAD, D])
        fstats = sb("fstats", [P, QUAD, 6])
        fmv = sb("fmv", [P, QUAD, 2])
        fve = sb("fve", [P, QUAD])
        frs = sb("frs", [P, QUAD])

        psQK = ps("psQK", [P, 2, BANK])
        psV = ps("psV", [P, BANK])
        psT0 = ps("psT0", [P, 4, P])
        psT1 = ps("psT1", [P, 4, P])
        psS = ps("psS", [P, 2, BANK])
        psM = ps("psM", [P, BANK])
        tin = psT0[:, 0, :]
        scores = psS[:, :, 0:4 * KEYS].rearrange("p r (c k) -> p r c k", c=4)
        pair = [psS, psQK]
        shifted_at = [psQK[:, 0, 0:QUAD * HALF], psQK[:, 1, 0:QUAD * HALF]] + 2 * [psV[:, 0:QUAD * HALF]]

        ld_c, ld_attn, ld_ffn = sem("ld_c"), sem("ld_attn"), sem("ld_ffn")
        stats_done, ln_step, rstd_done = sem("stats_done"), sem("ln_step"), sem("rstd_done")
        zeroed, tab_done, tab_ready = sem("zeroed"), sem("tab_done"), sem("tab_ready")
        layer_in, attn_out = sem("layer_in"), sem("attn_out")
        yin_ready, t_done, xs_ready = sem("yin_ready"), sem("t_done"), sem("xs_ready")
        qk_proj, v_proj, v_ready = sem("qk_proj"), sem("v_proj"), sem("v_ready")
        sq_done, ss_done, rn_done = sem("sq_done"), sem("ss_done"), sem("rn_done")
        raw_done, tc_done, ts_done = sem("raw_done"), sem("tc_done"), sem("ts_done")
        rs_done, qr_done = sem("rs_done"), sem("qr_done")
        qT_done, qT_ready, kT_done, kT_ready = sem("qT_done"), sem("qT_ready"), sem("kT_done"), sem("kT_ready")
        s_done, mx_done, sd_done, exp_done = sem("s_done"), sem("mx_done"), sem("sd_done"), sem("exp_done")
        pT0_done, pT0_ready = sem("pT0_done"), sem("pT0_ready")
        pT1_done, pT1_ready = sem("pT1_done"), sem("pT1_ready")
        den_done, rden_done, norm_done, pr_done = sem("den_done"), sem("rden_done"), sem("norm_done"), sem("pr_done")
        pv_done, oT_ready, wo_done = sem("pv_done"), sem("oT_ready"), sem("wo_done")
        sh_done, fxs_ready, fstat, fve_done = sem("sh_done"), sem("fxs_ready"), sem("fstat"), sem("fve_done")
        frs_done, fxn_done, fT_done, fT_ready = sem("frs_done"), sem("fxn_done"), sem("fT_done"), sem("fT_ready")
        up_done, gate_done, hid_done = sem("up_done"), sem("gate_done"), sem("hid_done")
        down_done, yb_done, x_done = sem("down_done"), sem("yb_done"), sem("x_done")

        block = ctx.enter_context(nc.Block())

        @block.sync
        def _(sp):
            for dst, name in ((rot, "c_rot"), (mask_in, "c_mask"), (shift, "c_shift")):
                sp.dma_start(dst[:], io[name]).then_inc(ld_c, 16)
            sp.dma_start(scales[:, :, :, :], io["l_scales"].partition_broadcast(P)).then_inc(ld_c, 16)

            def load_attn(l):
                sp.dma_start(w_qkv[:, :], io["L1_ffn_Wqkv"][one(l), :, :].rearrange("o k n -> k (o n)"))\
                  .then_inc(ld_attn, 16)
                sp.dma_start(w_o[:, :, :], io["L1_ffn_Wo"][one(l), :, :].rearrange("o (c k) n -> k (o c) n", k=P))\
                  .then_inc(ld_attn, 16)

            def load_ffn(l):
                sp.dma_start(w1[:, :, :], io["l_w1"][one(l), :, :, :].rearrange("o k c n -> k (o c) n"))\
                  .then_inc(ld_ffn, 16)
                sp.dma_start(w2[:, :, :], io["l_w2"][one(l), :, :, :].rearrange("o k c n -> k (o c) n"))\
                  .then_inc(ld_ffn, 16)
                sp.dma_start(cols[:, :], io["l_cols"][one(l), :, :].rearrange("o k n -> k (o n)")).then_inc(ld_ffn, 16)
                sp.dma_start(b2[:, :], io["L1_ffn_b2"][one(l), :].rearrange("o n -> (o n)").partition_broadcast(P))\
                  .then_inc(ld_ffn, 16)

            load_attn(0)
            load_ffn(0)
            with sp.Fori(1, LAYERS) as l:
                sp.wait_ge(wo_done, l * B)
                load_attn(l)
                sp.wait_ge(layer_in, l * B + B)
                load_ffn(l)

        @block.gpsimd
        def _(pool):
            pool.memset(kT[:, :, 0:WINDOW], 0.0).then_inc(zeroed, 1)
            pool.memset(pr[:, :, :, :, :], 0.0).then_inc(zeroed, 1)
            pool.memset(mhalf[:, :], -0.5).then_inc(zeroed, 1)
            ln_rstd_pool(pool, c, ln_step, rstd_done)
            pool.wait_ge(ld_c, 16 * 4)
            pool.wait_ge(zeroed, 6)
            with pool.Fori(0, LAYERS) as l:
                batches, steps, quads = l * B, l * UNITS, l * QUADS

                sc = scales[:, one(l), :, :].rearrange("p o a d -> p (o a) d")
                pool.tensor_tensor(tab[:, 0:2, :], rot[:, 0:2, :], sc, ALU.mult).then_inc(tab_done, 1)
                for to, frm in ((0, DH // 2), (DH // 2, 0)):
                    pool.tensor_tensor(tab[:, 2:4, to:to + DH // 2], rot[:, 2:4, to:to + DH // 2],
                                       sc[:, :, frm:frm + DH // 2], ALU.mult).then_inc(tab_done, 1)
                pool.wait_ge(tab_done, l * 3 + 3)

                def body(b, i, s, live):
                    u = s % 2
                    if live(0):
                        pool.wait_ge(raw_done, steps + i + 1)
                        for to, frm in ((0, DH // 2), (DH // 2, 0)):
                            t = tab[:, 2:4, to:to + DH // 2].unsqueeze(2).to_broadcast([P, 2, UH, DH // 2])
                            pool.tensor_tensor(
                                ts[:, u, :, to:to + DH // 2].rearrange("p (a h) d -> p a h d", a=2),
                                raw[:, u, :, frm:frm + DH // 2].rearrange("p (a h) d -> p a h d", a=2),
                                t, ALU.mult).then_inc(ts_done, 1)
                        pool.wait_ge(ss_done, steps + i + 1)
                        pool.tensor_tensor(rn[:, u, :], ss[:, u, :], mhalf[:, :], ALU.pow).then_inc(rn_done, 1)

                units(pool, body, 0)
                pool.wait_ge(ld_ffn, l * 64 + 64)

                def rstd(q):
                    pool.wait_ge(fve_done, quads + q + 1)
                    pool.tensor_tensor(frs[:, :], fve[:, :], mhalf[:, 0:QUAD], ALU.pow).then_inc(frs_done, 1)

                rstd(0)
                rstd(1)
                pool.wait_ge(attn_out, batches + B + 1)
                for q in range(QUADS):
                    if q >= 1:
                        pool.wait_ge(layer_in, batches + B + QUAD * q)
                    pool.tensor_tensor(yb[:, :, :], Y[:, QUAD * q:QUAD * q + QUAD, :],
                                       b2[:, :].unsqueeze(1).to_broadcast([P, QUAD, D]), ALU.add)\
                        .then_inc(yb_done, 1)
                    if q + 2 < QUADS:
                        rstd(q + 2)

        @block.vector
        def _(dve):
            dve.memset(xsT[HALF:, 0:1], 0.0).then_inc(zeroed, 1)
            dve.memset(den[:, :], 1.0).then_inc(attn_out, 1)
            dve.wait_ge(ld_c, 16 * 4)
            dve.tensor_copy(mask[:, :].rearrange("p (c k) -> p c k", c=4),
                            mask_in[:, :].unsqueeze(1).to_broadcast([P, 4, KEYS])).then_inc(zeroed, 1)
            dve.tensor_copy(ident_bf[:, :], c.ident[:, :]).then_inc(zeroed, 1)
            ln_stats_dve(dve, c, stats_done, ln_step, X)
            dve.wait_ge(rstd_done, 2)
            for b in range(B):
                dve.tensor_scalar(Y[:, b, :], X[:, b, :], c.meanvar[:, b, 0:1], c.rstd[:, b:b + 1],
                                  ALU.subtract, ALU.mult).then_inc(layer_in, 1)
            dve.wait_ge(zeroed, 6)
            dve.wait_ge(layer_in, B)
            dve.tensor_scalar(y_in[:, :], Y[:, 0, :], 1.0, None, ALU.mult).then_inc(yin_ready, 1)
            with dve.Fori(0, LAYERS) as l:
                batches, steps, quads = l * B, l * UNITS, l * QUADS

                def stage(b):
                    dve.tensor_scalar(y_in[:, :], row(Y[:, one(b), :]), 1.0, None, ALU.mult).then_inc(yin_ready, 1)

                dve.wait_ge(tab_done, l * 3 + 3)

                def rotated(j, t):
                    dve.wait_ge(rs_done, steps + j + 1)
                    dve.wait_ge(rn_done, steps + j + 1)
                    dve.scalar_tensor_tensor(out=qr[:, t, :].rearrange("p (h d) -> p h d", d=DH),
                                             in0=rn[:, t, :].unsqueeze(2).to_broadcast([P, 2 * UH, DH]),
                                             scalar=1e12, in1=rs[:, :, :],
                                             op0=ALU.min, op1=ALU.mult).then_inc(qr_done, 1)

                def body(b, i, s, live):
                    u = s % 2
                    if live(1):
                        rotated(i - 1, 1 - u)
                    if live(2):
                        dve.wait_ge(exp_done, steps + i - 1)
                        dve.tensor_reduce(den[:, :], sd[:, u, :, :, :].rearrange("p r c k -> p (r c) k"),
                                          AX.X, ALU.add).then_inc(den_done, 1)
                        dve.wait_ge(den_done, steps + i - 1)
                        dve.reciprocal(rden[:, :], den[:, :]).then_inc(rden_done, 1)
                        dve.wait_ge(rden_done, steps + i - 1)
                        e = sd[:, u, :, :, :].rearrange("p r c k -> p (r c) k")
                        dve.tensor_tensor(e, e, rden[:, :].unsqueeze(2).to_broadcast([P, UH, KEYS]), ALU.mult)\
                           .then_inc(norm_done, 1)
                    if live(0):
                        if u == 1 and live(-1):
                            dve.wait_ge(t_done, batches + b + 1)
                            stage(b + 1)
                        dve.wait_ge(raw_done, steps + i + 1)
                        dve.tensor_tensor(tc[:, u, :, :].rearrange("p (a h) d -> p a h d", a=2),
                                          raw[:, u, :, :].rearrange("p (a h) d -> p a h d", a=2),
                                          tab[:, 0:2, :].unsqueeze(2).to_broadcast([P, 2, UH, DH]),
                                          ALU.mult).then_inc(tc_done, 1)
                        dve.wait_ge(sq_done, steps + i + 1)
                        dve.tensor_reduce(ss[:, u, :], sq[:, :, :], AX.X, ALU.add).then_inc(ss_done, 1)
                    if live(4) and u == 1:
                        dve.wait_ge(wo_done, batches + b - 1)
                        dve.tensor_tensor(row(Y[:, one(b - 2), :]), psM[:, 0:D], row(Y[:, one(b - 2), :]),
                                          ALU.add).then_inc(attn_out, 1)
                    if live(0):
                        dve.wait_ge(tc_done, steps + i + 1)
                        dve.wait_ge(ts_done, steps * 2 + i * 2 + 2)
                        dve.tensor_tensor(rs[:, :, :].rearrange("p h d -> p (h d)"),
                                          tc[:, u, :, :].rearrange("p h d -> p (h d)"),
                                          ts[:, u, :, :].rearrange("p h d -> p (h d)"), ALU.add).then_inc(rs_done, 1)
                    if live(1):
                        v = (s - 1) % 2
                        if live(3):
                            dve.wait_ge(pr_done, steps * 4 + i * 4 - 8)
                        for r in range(2):
                            dve.wait_ge(s_done, steps * 2 + i * 2 - 1 + r)
                            dve.tensor_reduce(mx[:, r, :], scores[:, r, :, :], AX.X, ALU.max).then_inc(mx_done, 1)
                            dve.wait_ge(mx_done, steps * 2 + i * 2 - 1 + r)
                            dve.tensor_tensor(sd[:, v, r, :, :], scores[:, r, :, :],
                                              mx[:, r, :].unsqueeze(2).to_broadcast([P, 4, KEYS]),
                                              ALU.subtract).then_inc(sd_done, 1)

                def moments(q):
                    dve.wait_ge(fxs_ready, quads * 2 + 2 * q + 2)
                    for t in range(QUAD):
                        dve.bn_stats(fstats[:, t, :], xs[:, q % 2, t, :]).then_inc(fstat, 1)
                    dve.wait_ge(fstat, quads * 8 + 8 * q + 4)
                    dve.memset(fve[:, :], 0.0)
                    for t in range(QUAD):
                        dve.bn_aggr(fmv[:, t, :], fstats[:, t, :]).then_inc(fstat, 1)
                    dve.wait_ge(fstat, quads * 8 + 8 * q + 8)
                    dve.tensor_scalar(fve[:, :], fmv[:, :, 1], LN_EPS, None, ALU.add).then_inc(fve_done, 1)

                def normalize(q):
                    dve.wait_ge(frs_done, quads + q + 1)
                    for t in range(QUAD):
                        dve.tensor_scalar(xn[:, q % 2, t, :], xs[:, q % 2, t, :], fmv[:, t, 0:1], frs[:, t:t + 1],
                                          ALU.subtract, ALU.mult).then_inc(fxn_done, 1)

                def affine(q):
                    dve.wait_ge(fT_done, quads + q + 1)
                    dve.tensor_scalar(xnT[:, q % 2, :], psT0[:, :, :].rearrange("p t n -> p (t n)"), cols[:, 6:7],
                                      cols[:, 7:8], ALU.mult, ALU.add).then_inc(fT_ready, 1)

                def hidden(q, ch):
                    n = 3 * q + ch
                    dve.wait_ge(gate_done, quads * 3 + n + 1)
                    dve.scalar_tensor_tensor(out=hid[:, q % 2, ch, :], in0=pair[n % 2][:, 0, :],
                                             scalar=cols[:, ch:ch + 1], in1=gate[:, n % 2, :],
                                             op0=ALU.add, op1=ALU.mult).then_inc(hid_done, 1)

                def result(q):
                    dve.wait_ge(down_done, quads + q + 1)
                    dve.wait_ge(yb_done, quads + q + 1)
                    dve.tensor_tensor(Y[:, QUAD * q:QUAD * q + QUAD, :].rearrange("p t n -> p (t n)"), psM[:, :],
                                      yb[:, :, :].rearrange("p t n -> p (t n)"), ALU.add)\
                       .then_inc(layer_in, QUAD)

                def first_quads():
                    moments(0)
                    normalize(0)
                    moments(1)

                units(dve, body, 4, {UNITS + 2: first_quads})

                dve.wait_ge(ld_ffn, l * 64 + 64)
                affine(0)
                for q in range(QUADS):
                    hidden(q, 0)
                    if q + 1 < QUADS:
                        normalize(q + 1)
                    if q >= 1:
                        result(q - 1)
                    if q + 2 < QUADS:
                        moments(q + 2)
                    hidden(q, 1)
                    if q + 1 < QUADS:
                        affine(q + 1)
                    hidden(q, 2)
                dve.wait_ge(t_done, batches + B)
                dve.wait_ge(layer_in, batches + B + QUAD)
                dve.tensor_scalar(y_in[:, :], Y[:, 0, :], 1.0, None, ALU.mult).then_inc(yin_ready, 1)
                result(QUADS - 1)

            dve.wait_ge(layer_in, B + LAYERS * B)
            dve.tensor_tensor(X[:, :, :], X[:, :, :], Y[:, :, :], ALU.add).then_inc(x_done, 1)
            dve.wait_ge(x_done, 1)

        @block.scalar
        def _(act):
            act.wait_ge(zeroed, 6)

            def evac_in(n):
                act.wait_ge(t_done, n + 1)
                act.activation(xsT[0:HALF, :], tin[0:HALF, :], ACT.Copy).then_inc(xs_ready, 1)
                act.activation(xsT[HALF:, 1:P], tin[HALF:, 0:P - 1], ACT.Copy).then_inc(xs_ready, 1)

            evac_in(0)
            with act.Fori(0, LAYERS) as l:
                batches, steps, quads = l * B, l * UNITS, l * QUADS

                def body(b, i, s, live):
                    u = s % 2
                    if live(2):
                        act.wait_ge(sd_done, steps * 2 + i * 2 - 2)
                        e = sd[:, u, :, :, :].rearrange("p r c k -> p (r c k)")
                        act.activation(e, e, ACT.Exp).then_inc(exp_done, 1)
                    if live(0):
                        act.wait_ge(qk_proj, steps + i + 1)
                        if live(2):
                            act.wait_ge(rs_done, steps + i - 1)
                        act.activation(raw[:, u, :, :], psQK[:, :, :].rearrange("p a (h d) -> p (a h) d", h=UH),
                                       ACT.Copy).then_inc(raw_done, 1)
                    if live(3):
                        act.wait_ge(pT1_done, steps + i - 2)
                        act.activation(prT[:, 0, :, :], psT1[:, :, :], ACT.Copy).then_inc(pT1_ready, 1)
                        act.wait_ge(pT0_done, steps + i - 2)
                        act.activation(prT[:, 1, :, :], psT0[:, :, :], ACT.Copy).then_inc(pT0_ready, 1)
                    if live(0):
                        act.wait_ge(v_proj, steps + i + 1)
                        act.activation(v1[:, s, :, :], psV[:, :].rearrange("p (n d) -> p n d", d=DH),
                                       ACT.Copy).then_inc(v_ready, 1)
                        if live(1):
                            act.wait_ge(ss_done, steps + i)
                        act.activation(sq[:, :, :], psQK[:, :, :].rearrange("p a (h d) -> p (a h) d", h=UH),
                                       ACT.Square).then_inc(sq_done, 1)
                    if live(1):
                        act.wait_ge(kT_done, steps + i)
                        act.activation(kT[:, :, WINDOW:], psT1[:, :, :], ACT.Copy).then_inc(kT_ready, 1)
                        act.wait_ge(qT_done, steps + i)
                        act.activation(qT[:, :, :], psT0[:, :, :], ACT.Copy).then_inc(qT_ready, 1)
                    if live(3):
                        act.wait_ge(pv_done, steps + i - 2)
                        w = (s - 3) % 2
                        act.activation(oT[:, 4 * w:4 * w + 4, :].rearrange("p c q -> p (c q)"), psV[:, :], ACT.Copy)\
                           .then_inc(oT_ready, 1)
                    if live(0) and u == 1 and live(-1):
                        evac_in(batches + b + 1)
                    if live(2):
                        act.wait_ge(norm_done, steps + i - 1)
                        for w in range(WINDOWS):
                            r, lo = slice(WINDOW * w, WINDOW * w + WINDOW), max(0, WINDOW * (w - 1))
                            hi = WINDOW * (w + 1)
                            act.activation(pr[r, u, :, :, lo:hi].rearrange("p r c k -> p (r c) k"),
                                           sd[r, u, :, :, KEYS - (hi - lo):].rearrange("p r c k -> p (r c) k"),
                                           ACT.Copy).then_inc(pr_done, 1)

                def shifted(q):
                    v = q % 2
                    if q >= 2:
                        act.wait_ge(fxn_done, batches + QUAD * (q - 1))
                        act.wait_ge(attn_out, batches + B + 1)
                    else:
                        act.wait_ge(attn_out, batches + QUAD * q + QUAD + 1)
                    act.activation(xs[:, v, :, 0:HALF], Y[:, QUAD * q:QUAD * q + QUAD, 0:HALF], ACT.Copy)\
                       .then_inc(fxs_ready, 1)
                    act.wait_ge(sh_done, quads + q + 1)
                    act.activation(xs[:, v, :, HALF:], shifted_at[q].rearrange("p (t n) -> p t n", t=QUAD),
                                   ACT.Copy).then_inc(fxs_ready, 1)

                def first_quads():
                    shifted(0)
                    shifted(1)

                units(act, body, 3, {UNITS + 1: first_quads})

                act.wait_ge(ld_ffn, l * 64 + 64)
                for q in range(QUADS):
                    for ch in range(3):
                        n = 3 * q + ch
                        act.wait_ge(up_done, quads * 3 + n + 1)
                        if n >= 2:
                            act.wait_ge(hid_done, quads * 3 + n - 1)
                        act.activation(gate[:, n % 2, :], pair[n % 2][:, 1, :], ACT.Gelu, bias=cols[:, 3 + ch:4 + ch])\
                           .then_inc(gate_done, 1)
                        if ch == 0 and q + 2 < QUADS:
                            shifted(q + 2)
                evac_in(batches + B)

        @block.tensor
        def _(pe):
            pe.wait_ge(ld_c, 16 * 4)
            pe.wait_ge(zeroed, 6)

            def transpose_in(n):
                pe.wait_ge(yin_ready, n + 1)
                pe.transpose(tin, y_in[:, :], c.ident[:, :]).then_inc(t_done, 1)

            transpose_in(0)
            with pe.Fori(0, LAYERS) as l:
                batches, steps, quads = l * B, l * UNITS, l * QUADS
                pe.wait_ge(ld_attn, l * 32 + 32)

                def body(b, i, s, live):
                    u = s % 2
                    if live(0):
                        pe.wait_ge(xs_ready, batches * 2 + b * 2 + 2)
                        if live(1):
                            pe.wait_ge(sq_done, steps + i)
                        for qk in range(2):
                            at = INNER * qk + UH * DH * u
                            mm = pe.matmul(psQK[:, qk, :], xsT[:, :], w_qkv[:, at:at + UH * DH],
                                           start=True, stop=True)
                        mm.then_inc(qk_proj, 1)
                    if live(3):
                        v = (s - 3) % 2
                        pe.wait_ge(pr_done, steps * 4 + i * 4 - 8)
                        for ch in range(4):
                            mm = pe.transpose(psT1[:, ch, :], pr[:, v, 0, ch, :], c.ident[:, :])
                        mm.then_inc(pT1_done, 1)
                        for ch in range(4):
                            mm = pe.transpose(psT0[:, ch, :], pr[:, v, 1, ch, :], c.ident[:, :])
                        mm.then_inc(pT0_done, 1)
                    if live(0):
                        if live(4):
                            pe.wait_ge(oT_ready, steps + i - 3)
                        elif live(1):
                            pe.wait_ge(v_ready, steps + i)
                        at = 2 * INNER + UH * DH * u
                        pe.matmul(psV[:, :], xsT[:, :], w_qkv[:, at:at + UH * DH], start=True, stop=True)\
                          .then_inc(v_proj, 1)
                    if live(4):
                        pe.wait_ge(oT_ready, steps + i - 3)
                        if u == 0:
                            pe.wait_ge(attn_out, batches + b - 1)
                        for ch in range(4):
                            mm = pe.matmul(psM[:, 0:D], oT[:, 4 * u + ch, :], w_o[:, 4 * u + ch, :],
                                           start=(u == 0 and ch == 0), stop=(u == 1 and ch == 3))
                        if u == 1:
                            mm.then_inc(wo_done, 1)
                    if live(1):
                        v = (s - 1) % 2
                        pe.wait_ge(qr_done, steps + i)
                        if live(3):
                            pe.wait_ge(pT1_ready, steps + i - 2)
                        for ch in range(4):
                            mm = pe.transpose(psT1[:, ch, :], qr[:, v, 512 + P * ch:512 + P * ch + P], c.ident[:, :])
                        mm.then_inc(kT_done, 1)
                        if live(3):
                            pe.wait_ge(pT0_ready, steps + i - 2)
                        for ch in range(4):
                            mm = pe.transpose(psT0[:, ch, :], qr[:, v, P * ch:P * ch + P], c.ident[:, :])
                        mm.then_inc(qT_done, 1)
                    if live(3):
                        q = (s - 3) % 4
                        pe.wait_ge(pT0_ready, steps + i - 2)
                        pe.wait_ge(pT1_ready, steps + i - 2)
                        if live(0):
                            pe.wait_ge(v_ready, steps + i + 1)
                        if live(4):
                            pe.wait_ge(oT_ready, steps + i - 3)
                        for ch in range(4):
                            for r in range(2):
                                mm = pe.matmul(psV[DH * r:DH * r + DH, P * ch:P * ch + P], v1[:, q, 2 * ch + r, :],
                                               prT[:, r, ch, :], start=True, stop=True)
                        mm.then_inc(pv_done, 1)
                    if live(0) and u == 1 and live(-1):
                        pe.wait_ge(qT_ready, steps + i)
                        transpose_in(batches + b + 1)
                    if live(1):
                        pe.wait_ge(kT_ready, steps + i)
                        pe.wait_ge(qT_ready, steps + i)
                        if live(2):
                            pe.wait_ge(sd_done, steps * 2 + i * 2 - 2)
                        for r in range(2):
                            pe.matmul(psS[:, r, 0:4 * KEYS], ident_bf[:, :], mask[:, :], start=True, stop=False,
                                      skip_group_check=True)
                            rows = slice(DH * r, DH * r + DH)
                            for ch in range(4):
                                for w in range(WINDOWS):
                                    mm = pe.matmul(psS[WINDOW * w:WINDOW * w + WINDOW, r, KEYS * ch:KEYS * ch + KEYS],
                                                   qT[rows, ch, WINDOW * w:WINDOW * w + WINDOW],
                                                   kT[rows, ch, WINDOW * w:WINDOW * w + KEYS],
                                                   start=False, stop=True, skip_group_check=True)
                            mm.then_inc(s_done, 1)
                def shift_tokens(q):
                    if q == 0:
                        pe.wait_ge(sq_done, steps + UNITS)
                        pe.wait_ge(attn_out, batches + 2 * QUAD + 1)
                    elif q == 3:
                        pe.wait_ge(fxs_ready, quads * 2 + 2 * q)
                    pe.matmul(shifted_at[q], shift[:, :], Y[:, QUAD * q:QUAD * q + QUAD, HALF:],
                              start=True, stop=True).then_inc(sh_done, 1)

                def first_quads():
                    shift_tokens(0)
                    shift_tokens(1)

                units(pe, body, 4, {UNITS + 1: first_quads})

                def transposes(q):
                    pe.wait_ge(fxn_done, batches + QUAD * q + QUAD)
                    for t in range(QUAD):
                        mm = pe.transpose(psT0[:, t, :], xn[:, q % 2, t, :], c.ident[:, :])
                    mm.then_inc(fT_done, 1)

                def up(q, ch):
                    n = 3 * q + ch
                    if ch == 0:
                        pe.wait_ge(fT_ready, quads + q + 1)
                    if n == 1:
                        pe.wait_ge(fxs_ready, quads * 2 + 4)
                    if n >= 2:
                        pe.wait_ge(hid_done, quads * 3 + n - 1)
                    for part in range(2):
                        mm = pe.matmul(pair[n % 2][:, part, :], w1[:, 3 * part + ch, :], xnT[:, q % 2, :],
                                       start=True, stop=True)
                    mm.then_inc(up_done, 1)

                def down(q):
                    pe.wait_ge(hid_done, quads * 3 + 3 * q + 3)
                    if q >= 1:
                        pe.wait_ge(layer_in, batches + B + QUAD * q)
                    for t in range(QUAD):
                        for ch in range(3):
                            mm = pe.matmul(psM[:, P * t:P * t + P], hid[:, q % 2, ch, P * t:P * t + P], w2[:, ch, :],
                                           start=(ch == 0), stop=(ch == 2))
                    mm.then_inc(down_done, 1)

                pe.wait_ge(ld_ffn, l * 64 + 64)
                transposes(0)
                pe.wait_ge(attn_out, batches + B + 1)
                for q in range(QUADS):
                    up(q, 0)
                    if q >= 1:
                        down(q - 1)
                    if q + 2 < QUADS:
                        shift_tokens(q + 2)
                    up(q, 1)
                    if q + 1 < QUADS:
                        transposes(q + 1)
                    up(q, 2)
                transpose_in(batches + B)
                down(QUADS - 1)


def store(c, src):
    with ExitStack() as ctx:
        stored = c.sem("stored")
        block = ctx.enter_context(c.nc.Block())

        @block.sync
        def _(sp):
            sp.dma_start(c.io["out"].rearrange("b t d -> t b d"), src).then_inc(stored, 16)
            sp.wait_ge(stored, 16)


STAGES = [first_attention, expert_ffn, second_attention, local_transformer]


def program(nc, io, upto=9):
    with ExitStack() as ctx:
        c = Core(nc, ctx, io)
        for stage in STAGES[:upto]:
            stage(c)
        store(c, c.X[:, :, :])


def constants():
    f = np.float32
    half = np.arange(0, DH, 2, dtype=f)
    t = np.arange(P, dtype=f)
    freqs = t[:, None] * (f(1.0) / f(10000.0) ** (half / f(DH)))[None, :]
    freqs = np.concatenate([freqs, freqs], -1).astype(f)
    base = (half + f(0.4 * DH)) / f(1.4 * DH)
    scale = base[None, :] ** ((t - P // 2) / f(WINDOW // 2))[:, None]
    scale = np.concatenate([scale, scale], -1).astype(f)
    sign = np.where(np.arange(DH) < DH // 2, f(-1.0), f(1.0))
    cos, sin = np.cos(freqs), np.sin(freqs) * sign
    rot = np.stack([cos * scale * f(QK_SCALE), cos / scale, sin * scale * f(QK_SCALE), sin / scale], 1)
    query = np.arange(P)[:, None]
    key = query // WINDOW * WINDOW - WINDOW + np.arange(2 * WINDOW)[None, :]
    masked = (query < key) | (query > key + WINDOW) | (key < 0)
    mask = np.where(masked, f(-3.0e38), f(0.0))
    return {
        "c_ident": np.eye(P, dtype=f),
        "c_shift": np.eye(P, k=1, dtype=f),
        "c_before": np.triu(np.ones((P, P), f), 1),
        "c_lower": np.tril(np.ones((EXPERTS, EXPERTS), f), -1),
        "c_mask": mask,
        "c_rot": rot.astype(f),
    }


def laid_out(inputs):
    w0 = np.zeros((P, 2, 4, 4, 32), np.float32)
    b0 = np.zeros((4, 32, 2, 2, 2), np.float32)
    for qk, name in enumerate("qk"):
        w0[:, qk, :, :, :DEPTH0] = np.asarray(inputs["L0_xattn_W" + name]).reshape(D, 4, 4, DEPTH0)
        b0[:, :DEPTH0, :, qk, :] = np.asarray(inputs["L0_xattn_b" + name]).reshape(2, 2, 4, DEPTH0).transpose(2, 3, 0, 1)
    def padded(a, axis):
        a = np.asarray(a)
        shape = list(a.shape)
        shape[axis] = 3 * P
        out = np.zeros(shape, a.dtype)
        out[tuple(slice(n) for n in a.shape)] = a
        return out

    w1 = np.asarray(inputs["L1_ffn_W1"]).reshape(LAYERS, D, 2, GLU)
    b1 = np.asarray(inputs["L1_ffn_b1"]).reshape(LAYERS, 2, GLU)
    cols = np.concatenate([padded(b1, 2).reshape(LAYERS, 6, P), np.asarray(inputs["L1_ffn_ln_g"])[:, None],
                           np.asarray(inputs["L1_ffn_ln_b"])[:, None]], 1)
    local = {
        "l_w1": padded(w1, 3).reshape(LAYERS, D, 6, P),
        "l_w2": padded(inputs["L1_ffn_W2"], 1).reshape(LAYERS, 3, P, D).transpose(0, 2, 1, 3),
        "l_cols": cols.transpose(0, 2, 1),
        "l_scales": np.stack([inputs["L1_ffn_q_scale"], inputs["L1_ffn_k_scale"]], 1),
    }
    local["l_wr"] = np.asarray(inputs["L0_ffn_Wr"]).T
    local["l_w1x"] = np.stack([np.asarray(inputs["L1_xattn_W" + n]).T for n in "qkvo"], 1)
    local["l_b1x"] = np.stack([inputs["L1_xattn_bq"], inputs["L1_xattn_bk"]], 1)
    return {**local, "l_w0_pad": w0.reshape(P, 2, 4, P), "l_b0_pad": b0.reshape(P, 2, 2, 2)}


def kernel(**inputs):
    import concourse.bacc as _bacc
    from concourse.bass_utils import run_bass_kernel_spmd as _run

    nc = _bacc.Bacc("TRN2", target_bir_lowering=False, num_devices=1)
    arrays, io = {}, {}
    for name, a in {**inputs, **laid_out(inputs), **constants()}.items():
        a = np.ascontiguousarray(a)
        arrays["in_" + name] = a
        io[name] = nc.dram_tensor("in_" + name, a.shape, mybir.dt.from_np(a.dtype), kind="ExternalInput").ap()
    io["out"] = nc.dram_tensor("out", (B, P, D), F32, kind="ExternalOutput").ap()
    program(nc, io)
    return _run(nc, [arrays], core_ids=[0]).results[0]["out"]
```
